# Optimizing a Trainium2 kernel written in Bass

```python
import numpy as np
import jax
import jax.numpy as jnp

def _softmax(x, axis=-1):
    return jax.nn.softmax(x, axis=axis)

def _gelu(x):
    return jax.nn.gelu(x, approximate=True)

def _silu(x):
    return jax.nn.silu(x)

def _sigmoid(x):
    return jax.nn.sigmoid(x)

def _layernorm(x, axis=-1, eps=1e-05):
    m = jnp.mean(x, axis=axis, keepdims=True)
    v = jnp.var(x, axis=axis, keepdims=True)
    return (x - m) / jnp.sqrt(v + eps)

def _scatter_add(tgt, idx, src, axis=0):
    return tgt.at[idx].add(src)

def _segment_sum(src, seg, n):
    return jax.ops.segment_sum(src, seg, n)
kernel_name = 'mk_seq_preln_d1_jaxref_r4_b1bb38'

def setup_inputs(seed: int=0):
    np.random.seed(seed)
    _w = jnp.asarray

    def _L0_attn_setup():
        import jax, jax.numpy as jnp
        import numpy as np
        B, N, D, H = (4, 1024, 256, 16)
        HD = D // H
        MLP = 4 * D

        def _ln(x, w, b):
            m = x.mean(-1, keepdims=True)
            v = x.var(-1, keepdims=True)
            return (x - m) / jnp.sqrt(v + 1e-05) * w + b
        key = jax.random.key(seed)
        ks = jax.random.split(key, 12)
        s = 1.0 / np.sqrt(D)
        sm = 1.0 / np.sqrt(MLP)
        return {'q_x': jax.random.normal(ks[0], (B, N, D), jnp.float32), 'ln1_w': jnp.ones((D,), jnp.float32), 'ln1_b': jnp.zeros((D,), jnp.float32), 'wq': jax.random.normal(ks[1], (D, D), jnp.float32) * s, 'bq': jnp.zeros((D,), jnp.float32), 'wk': jax.random.normal(ks[2], (D, D), jnp.float32) * s, 'bk': jnp.zeros((D,), jnp.float32), 'wv': jax.random.normal(ks[3], (D, D), jnp.float32) * s, 'bv': jnp.zeros((D,), jnp.float32), 'wo': jax.random.normal(ks[4], (D, D), jnp.float32) * s, 'bo': jnp.zeros((D,), jnp.float32), 'ln2_w': jnp.ones((D,), jnp.float32), 'ln2_b': jnp.zeros((D,), jnp.float32), 'fc_w': jax.random.normal(ks[5], (D, MLP), jnp.float32) * s, 'fc_b': jnp.zeros((MLP,), jnp.float32), 'proj_w': jax.random.normal(ks[6], (MLP, D), jnp.float32) * sm, 'proj_b': jnp.zeros((D,), jnp.float32)}
    _L0_attn_in = _L0_attn_setup()

    def _L0_ffn_setup():
        import jax, jax.numpy as jnp
        import numpy as np
        NEG_INF = -1e+30
        K = 2
        key = jax.random.key(seed)
        ks = jax.random.split(key, 5)
        B, S, D, O, E = (8, 512, 256, 256, 8)
        scale = 1.0 / np.sqrt(D)
        return {'x': jax.random.normal(ks[0], (B, S, D), dtype=jnp.float32), 'gate_w': jax.random.normal(ks[1], (E, D), dtype=jnp.float32) * scale, 'gate_b': jnp.zeros((E,), dtype=jnp.float32), 'expert_w': jax.random.normal(ks[2], (E, O, D), dtype=jnp.float32) * scale, 'expert_b': jnp.zeros((E, O), dtype=jnp.float32)}
    _L0_ffn_in = _L0_ffn_setup()
    _d = {'L0_attn_q_x': _L0_attn_in['q_x'], 'L0_attn_ln1_w': _L0_attn_in['ln1_w'], 'L0_attn_ln1_b': _L0_attn_in['ln1_b'], 'L0_attn_wq': _L0_attn_in['wq'], 'L0_attn_bq': _L0_attn_in['bq'], 'L0_attn_wk': _L0_attn_in['wk'], 'L0_attn_bk': _L0_attn_in['bk'], 'L0_attn_wv': _L0_attn_in['wv'], 'L0_attn_bv': _L0_attn_in['bv'], 'L0_attn_wo': _L0_attn_in['wo'], 'L0_attn_bo': _L0_attn_in['bo'], 'L0_attn_ln2_w': _L0_attn_in['ln2_w'], 'L0_attn_ln2_b': _L0_attn_in['ln2_b'], 'L0_attn_fc_w': _L0_attn_in['fc_w'], 'L0_attn_fc_b': _L0_attn_in['fc_b'], 'L0_attn_proj_w': _L0_attn_in['proj_w'], 'L0_attn_proj_b': _L0_attn_in['proj_b'], 'L0_ffn_gate_w': _L0_ffn_in['gate_w'], 'L0_ffn_gate_b': _L0_ffn_in['gate_b'], 'L0_ffn_expert_w': _L0_ffn_in['expert_w'], 'L0_ffn_expert_b': _L0_ffn_in['expert_b']}
    _x0 = _d['L0_attn_q_x']
    _d['L0_attn_q_x'] = jax.random.normal(jax.random.fold_in(jax.random.key(seed), 1), (4, 2048, 256), dtype=_x0.dtype)
    del _x0
    return _d

def reference(L0_attn_q_x, L0_attn_ln1_w, L0_attn_ln1_b, L0_attn_wq, L0_attn_bq, L0_attn_wk, L0_attn_bk, L0_attn_wv, L0_attn_bv, L0_attn_wo, L0_attn_bo, L0_attn_ln2_w, L0_attn_ln2_b, L0_attn_fc_w, L0_attn_fc_b, L0_attn_proj_w, L0_attn_proj_b, L0_ffn_gate_w, L0_ffn_gate_b, L0_ffn_expert_w, L0_ffn_expert_b):

    def _L0_attn_ref(q_x, ln1_w, ln1_b, wq, bq, wk, bk, wv, bv, wo, bo, ln2_w, ln2_b, fc_w, fc_b, proj_w, proj_b):
        import jax, jax.numpy as jnp
        import numpy as np
        B, N, D, H = (4, 1024, 256, 16)
        HD = D // H
        MLP = 4 * D

        def _ln(x, w, b):
            m = x.mean(-1, keepdims=True)
            v = x.var(-1, keepdims=True)
            return (x - m) / jnp.sqrt(v + 1e-05) * w + b
        b, n, c = q_x.shape
        xn = _ln(q_x, ln1_w, ln1_b)
        q = (xn @ wq + bq).reshape(b, n, H, HD).transpose(0, 2, 1, 3)
        k = (xn @ wk + bk).reshape(b, n, H, HD).transpose(0, 2, 1, 3)
        v = (xn @ wv + bv).reshape(b, n, H, HD).transpose(0, 2, 1, 3)
        fq = jax.nn.elu(q) + 1.0
        fk = jax.nn.elu(k) + 1.0
        kv = jnp.einsum('bhnd,bhne->bnde', fk, v)
        qkv = jnp.einsum('bhnd,bnde->bhne', fq, kv)
        k_sum = fk.sum(axis=1)
        qk = jnp.einsum('bhnd,bnd->bhn', fq, k_sum)
        attn = qkv / (qk[..., None] + 1e-06)
        attn = attn.transpose(0, 2, 1, 3).reshape(b, n, c)
        attn = attn @ wo + bo
        x = q_x + attn
        h = _ln(x, ln2_w, ln2_b)
        h = jax.nn.gelu(h @ fc_w + fc_b, approximate=False)
        return x + (h @ proj_w + proj_b)

    def _L0_ffn_ref(x, gate_w, gate_b, expert_w, expert_b):
        import jax, jax.numpy as jnp
        import numpy as np
        NEG_INF = -1e+30
        K = 2
        pooled = x.mean(axis=1)
        logits = pooled @ gate_w.T + gate_b
        topk_vals, _ = jax.lax.top_k(logits, K)
        min_topk = topk_vals[:, -1:]
        masked = jnp.where(logits < min_topk, -jnp.inf, logits)
        gates = jax.nn.softmax(masked, axis=-1)
        expert_out = jax.nn.gelu(jnp.einsum('bsd,eod->beso', x, expert_w) + expert_b[None, :, None, :], approximate=False)
        return jnp.einsum('be,beso->bso', gates, expert_out)
    x = L0_attn_q_x
    x = x + _L0_attn_ref(_layernorm(x, axis=-1), L0_attn_ln1_w, L0_attn_ln1_b, L0_attn_wq, L0_attn_bq, L0_attn_wk, L0_attn_bk, L0_attn_wv, L0_attn_bv, L0_attn_wo, L0_attn_bo, L0_attn_ln2_w, L0_attn_ln2_b, L0_attn_fc_w, L0_attn_fc_b, L0_attn_proj_w, L0_attn_proj_b)
    x = x + _L0_ffn_ref(_layernorm(x, axis=-1), L0_ffn_gate_w, L0_ffn_gate_b, L0_ffn_expert_w, L0_ffn_expert_b)
    return x

_drawn_inputs = setup_inputs


def setup_inputs(seed=0):
    import zlib

    import numpy as np

    out = dict(_drawn_inputs(seed))
    spreads = {'L0_attn_ln1_w': (1.0, 0.2),
     'L0_attn_ln1_b': (0.0, 0.672),
     'L0_attn_bq': (0.0, 0.8),
     'L0_attn_bk': (0.0, 0.8),
     'L0_attn_bv': (0.0, 0.591),
     'L0_attn_bo': (0.0, 0.1),
     'L0_attn_ln2_w': (1.0, 0.2),
     'L0_attn_ln2_b': (0.0, 0.1),
     'L0_attn_fc_b': (0.0, 0.1),
     'L0_attn_proj_b': (0.0, 0.1),
     'L0_ffn_gate_b': (0.0, 0.1),
     'L0_ffn_expert_b': (0.0, 0.35)}
    factors = {'L0_attn_wq': 3.303}
    for name, (base, spread) in spreads.items():
        noise = np.random.default_rng([zlib.crc32(name.encode()), seed]).standard_normal(out[name].shape)
        drawn = base * np.exp(spread * noise) if base else spread * noise
        out[name] = jnp.asarray(drawn.astype(out[name].dtype))
    for name, factor in factors.items():
        out[name] = (out[name] * factor).astype(out[name].dtype)
    return out
```

```python
import numpy as np
from contextlib import ExitStack

import concourse.bass as bass
from concourse import mybir

BATCH, SEQ, D = 4, 2048, 256
H, HD = 16, 16
MLP = 4 * D
E = 8
P = 128
NC = D // P
NM = MLP // P
T = 512
SUB = T // P
TILES = BATCH * SEQ // T
PER_BATCH = SEQ // T
RING = 4
NQ = 4
QT = T // NQ
TB = 4
GG = QT // TB
RG = 8
ROUNDS = GG // RG
EPS = 1e-5
DEN_EPS = 1e-6

LAG = {"L": 0, "D1": 0, "D2": 0, "B": 1, "A1": 2, "A2": 2, "C": 2, "E": 2, "F": 6}
FULL = ["L", "A1", "F", "A2", "B", "D1", "C", "D2", "E"]

INC = {
    "pt_full0": {"P": 1, "D2": 1, "B": 2, "C": 1, "E": 1, "F": 1, "G": 1},
    "pt_free0": {"P": 1, "D2": 1, "B": 2, "C": 1, "E": 1, "F": 1, "G": 1},
    "pt_full1": {"D2": 1, "B": 2, "C": 1, "E": 1, "F": 1},
    "pt_free1": {"D2": 1, "B": 2, "C": 1, "E": 1, "F": 1},
    "pq_full0": {"D2": 3, "B": 2, "A2": 1, "C": 5, "F": E},
    "pq_free0": {"D2": 3, "B": 2, "A2": 1, "C": 5, "F": E},
    "pq_full1": {"D2": 3, "B": 2, "A2": 1, "C": 5, "F": E},
    "pq_free1": {"D2": 3, "B": 2, "A2": 1, "C": 5, "F": E},
    "ps_full0": {"B": 4}, "ps_free0": {"B": 4},
    "ps_full1": {"B": 4}, "ps_free1": {"B": 4},
    "x_in": {"L": 16},
    "var_ready": {"D1": 1, "A2": 1, "C": 1},
    "rstd_ready": {"D1": 1, "A2": 1, "C": 1},
    "xhat_ready": {"D1": 1},
    "exp_ready": {"D2": 4},
    "feat_ready": {"D2": 4},
    "q_out": {"D2": 16}, "k_out": {"D2": 16}, "v_out": {"D2": 16},
    "q_in": {"D2": 64}, "k_in": {"D2": 64}, "v_in": {"D2": 128},
    "nd_out": {"B": 128}, "nd_in": {"B": 32},
    "attnT_ready": {"A1": 1},
    "y_ready": {"A2": 1}, "yb_ready": {"A2": 1}, "s_ready": {"P": 1, "A2": 1},
    "h_ready": {"A2": 1},
    "z_ready": {"C": 1},
    "pool_ready": {"G": 1}, "logit_ready": {"G": 1}, "gexp_ready": {"G": 1},
    "acc_ready": {"P": 1, "F": 2 * E},
    "out_stored": {"P": 16, "F": 16},
    "dve_chain": {"D1": 2, "A1": 2, "A2": 2, "C": 2, "G": 7},
    "pool_chain": {"A2": 1},
}


class Place:

    def __init__(self, stage, i, base, rates):
        self.stage, self.i, self.base, self.rates = stage, i, base, rates
        self.t = i - LAG[stage] if stage in LAG else None

    def at(self, name, more=0):
        value = self.base.get(name, 0) + more
        for index, rate in self.rates:
            if rate.get(name, 0):
                value = index * rate[name] + value
        return value


def total(stages):
    out = {}
    for name, by in INC.items():
        out[name] = sum(by.get(s, 0) for s in stages)
    return out


def plus(a, b, times=1):
    return {k: a.get(k, 0) + times * b.get(k, 0) for k in INC}


def walk(eng, run):
    base = total(["P"])

    def stages(names, i, rates):
        nonlocal base
        for s in names:
            run(Place(s, i, base, rates))
            base = plus(base, total([s]))

    def loop(lo, hi, names):
        nonlocal base
        rate = total(names)
        at = base
        with eng.Fori(0, hi - lo) as k:
            stages(names, k + lo, [(k, rate)])
        base = plus(at, rate, hi - lo)

    def drop(*out):
        return [s for s in FULL if s not in out]

    stages(["L", "D1", "D2"], 0, [])
    stages(["L", "B", "D1", "D2"], 1, [])
    loop(2, 6, drop("F"))
    at, rate, epoch = base, total(FULL), plus(total(["G"]), total(FULL), PER_BATCH)
    with eng.Fori(0, 2) as e:
        stages(["G"], 0, [(e, epoch)])
        with eng.Fori(0, PER_BATCH) as k:
            stages(FULL, e * PER_BATCH + k + 6, [(e, epoch), (k, rate)])
    base = plus(at, epoch, 2)
    stages(["G"], 0, [])
    loop(14, 16, FULL)
    stages(drop("L", "D1", "D2"), 16, [])
    stages(drop("L", "B", "D1", "D2"), 17, [])
    stages(["G"], 0, [])
    loop(18, 22, ["F"])


def build(nc, x, wqkv, wo, fcw, pjw, gw, ew, cols, rows, ident_d, mask_d, out):
    f32 = mybir.dt.float32
    ALU = mybir.AluOpType
    ACT = mybir.ActivationFunctionType
    AX = mybir.AxisListType.X

    ctx = ExitStack()
    with ctx:
        def sb(name, shape):
            return ctx.enter_context(nc.sbuf_tensor(name, shape, f32))

        def sem(name):
            return ctx.enter_context(nc.semaphore(name))

        w_qkv = sb("w_qkv", [P, 3, NC, D])
        w_o = sb("w_o", [P, NC, D])
        w_fc = sb("w_fc", [P, NC, MLP])
        w_pj = sb("w_pj", [P, NM, D])
        w_g = sb("w_g", [P, NC, E])
        w_e = sb("w_e", [P, E, NC, D])
        NCOL = 2 * 4 + 3 * NC + NM + E * NC
        col = sb("col", [P, NCOL])
        ln1w, ln1b, ln2w, ln2b = (col[:, NC * n:NC * (n + 1)] for n in range(4))
        b_qkv = col[:, 8:8 + 3 * NC]
        b_fc = col[:, 8 + 3 * NC:8 + 3 * NC + NM]
        b_e = col[:, 8 + 3 * NC + NM:NCOL]
        row = sb("row", [P, 2 * D + E])
        ident = sb("ident", [P, P])
        mask = sb("mask", [P, TB * H])
        mhalf = sb("mhalf", [P, 2 * SUB])
        x_sb = sb("x_sb", [P, RING, SUB, D])
        x2_sb = sb("x2_sb", [P, RING, SUB, D])
        zT = sb("zT", [P, RING, NC, T])
        pooled = sb("pooled", [P, NC, RING])
        mv1 = sb("mv1", [P, RING, SUB, 2])
        rs1 = sb("rs1", [P, RING, 2, SUB])
        stat = sb("stat", [P, SUB, 6])
        mv = sb("mv", [P, SUB, 2])
        var2 = sb("var2", [P, 2, SUB])
        rs = sb("rs", [P, SUB])
        xhat = sb("xhat", [P, SUB, D])
        hn = sb("hn", [P, SUB, D])
        z = sb("z", [P, SUB, D])
        xhT = sb("xhT", [P, NC, T])
        hT = sb("hT", [P, NC, T])
        expb = sb("expb", [P, 2, T])
        relub = sb("relub", [P, 2, T])
        feat = sb("feat", [P, 3, NC, T])
        out_sb = feat[:, 0].rearrange("p c t -> p (c t)").rearrange("p (s d) -> p s d", d=D)
        acc = feat[:, 1]
        ge = feat[:, 2]
        hid = sb("hid", [P, NM, T])
        qd = hid[:, 0:4].rearrange("p a b -> p (a b)").rearrange("p (h t) -> p h t", t=QT)
        kd = hid[:, 4:8].rearrange("p a b -> p (a b)").rearrange("p (h t) -> p h t", t=QT)
        vd = sb("vd", [P, 2, H, QT // 2])
        vb = sb("vb", [P, 2 * GG, 64])
        am = sb("am", [P, 2, 2, RG * 64])
        ot = sb("ot", [P, H, QT])
        nd = ot[:, :, :].rearrange("p h t -> p (h t)").rearrange("p (n c t) -> p n c t", n=2, c=NC)
        attnT = sb("attnT", [P, NC, T])
        x1 = sb("x1", [P, SUB, D])
        s_sb = sb("s_sb", [P, SUB, D])
        pb128 = sb("pb128", [P, NC, P])
        held_at = sb("held_at", [P, 1])
        g8 = sb("g8", [P, 6, E])
        gs = sb("gs", [P, 4])

        pt = [ctx.enter_context(nc.psum_tensor(f"pt{n}", [P, 512], f32)) for n in range(2)]
        pq = [ctx.enter_context(nc.psum_tensor(f"pq{n}", [P, 512], f32)) for n in range(2)]
        ps = [[ctx.enter_context(nc.psum_tensor(f"ps{n}{p}", [P, 512], f32)) for p in range(2)] for n in range(2)]

        qkv_dram = [nc.dram_tensor(f"scratch_{n}", (D, T), f32, kind="Internal").ap() for n in "qkv"]
        nd_dram = nc.dram_tensor("scratch_nd", (2, D, T), f32, kind="Internal").ap()

        S = {name: sem(name) for name in INC}
        w_in = [sem(f"w_in{n}") for n in range(10)]
        fold_done = sem("fold_done")
        const_done = sem("const_done")

        x_t = x.rearrange("(n s p) d -> n p s d", s=SUB, p=P)
        out_t = out.rearrange("(n s p) d -> n p s d", s=SUB, p=P)

        block = ctx.enter_context(nc.Block())

        held = sem("held")

        def waiter(eng, own=False):
            def wait(name, value):
                if not isinstance(value, int) or value > 0:
                    eng.wait_ge(S[name], value)
                    if own and not isinstance(value, int):
                        eng.sem_inc(held, 1)
            return wait

        @block.sync
        def _(sp):
            wait = waiter(sp, own=True)
            for n, (dst, src) in enumerate([
                (ident[:, :], ident_d), (col[:, :], cols), (w_qkv[:, :, :, :], wqkv), (row[:, :], rows),
                (mask[:, :], mask_d), (w_fc[:, :, :], fcw), (w_o[:, :, :], wo), (w_pj[:, :, :], pjw),
                (w_g[:, :, :], gw), (w_e[:, :, :, :], ew),
            ]):
                sp.dma_start(dst, src).then_inc(w_in[n], 16)

            def run(p):
                at = p.at
                if p.stage == "L":
                    wait("xhat_ready", at("xhat_ready"))
                    sp.dma_start(x_sb[:, p.t % RING], x_t[p.t]).then_inc(S["x_in"], 16)
                if p.stage == "D2":
                    for n, c in enumerate("qkv"):
                        wait(f"{c}_in", at(f"{c}_in"))
                        if n < 2:
                            wait("feat_ready", at("feat_ready", 2 * n + 2))
                        else:
                            for b in range(2):
                                wait(f"pq_free{b}", at(f"pq_free{b}", 3))
                        sp.dma_start(qkv_dram[n].rearrange("(c p) t -> p c t", p=P),
                                     feat[:, n]).then_inc(S[f"{c}_out"], 16)
                    wait("pq_full1", at("pq_full1"))
                    for n, (c, dst) in enumerate((("q", qd), ("k", kd))):
                        wait(f"{c}_out", at(f"{c}_out", 16))
                        src = qkv_dram[n].rearrange("(h d) t -> d h t", d=HD)
                        for q in range(NQ):
                            sp.dma_start(dst[32 * q:32 * q + HD], src[:, :, QT * q:QT * (q + 1)]).then_inc(S[f"{c}_in"], 16)
                    wait("v_out", at("v_out", 16))
                    if isinstance(p.t, int) and p.t == 0:
                        sp.wait_ge(const_done, 5)
                    for j in range(NQ):
                        src = qkv_dram[2].rearrange("(h d) (p b j t) -> p j b d h t", d=HD, p=2, b=2, j=2)
                        for b in range(2):
                            sp.dma_start(vd[32 * j:32 * j + HD, b], src[j // 2, j % 2, b]).then_inc(S["v_in"], 16)
                if p.stage == "B":
                    for b in range(2):
                        wait(f"pq_free{b}", at(f"pq_free{b}", ROUNDS // 2))
                    for q in range(NQ):
                        for n in range(2):
                            sp.dma_start(nd_dram[n].rearrange("(h e) t -> e h t", e=HD)[:, :, QT * q:QT * (q + 1)],
                                         ot[32 * q + HD * n:32 * q + HD * (n + 1)]).then_inc(S["nd_out"], 16)
                    wait("nd_out", at("nd_out", 128))
                    for n in range(2):
                        sp.dma_start(nd[:, n], nd_dram[n].rearrange("(c p) t -> p c t", p=P)).then_inc(S["nd_in"], 16)
                if p.stage == "F":
                    for u in range(2):
                        wait(f"pt_free{u}", at(f"pt_free{u}", 1))
                    sp.dma_start(out_t[p.t], out_sb).then_inc(S["out_stored"], 16)

            walk(sp, run)
            sp.wait_ge(S["out_stored"], 16 * (TILES + 1))

        @block.gpsimd
        def _(pool):
            wait = waiter(pool)
            nc.gpsimd.memset(mhalf[:, :], -0.5).then_inc(const_done, 1)
            nc.gpsimd.memset(vd[:, :, :, :], 0.0).then_inc(const_done, 1)
            nc.gpsimd.memset(vb[:, :, :], 0.0).then_inc(const_done, 1)
            pool.wait_ge(const_done, 3)
            nc.gpsimd.memset(vb[0:64, :, HD:2 * HD], 1.0).then_inc(const_done, 1)
            nc.gpsimd.memset(vb[64:128, :, 32 + HD:32 + 2 * HD], 1.0).then_inc(const_done, 1)
            pool.wait_ge(const_done, 5)
            pool.wait_ge(w_in[3], 16)

            pool.sem_inc(S["s_ready"], 1)
            pool.sem_inc(S["acc_ready"], 1)
            pool.sem_inc(S["out_stored"], 16)

            def rows_of(lo):
                return row[:, lo:lo + D].unsqueeze(1).broadcast_to([P, SUB, D])

            def run(p):
                at = p.at
                if p.stage == "D1":
                    wait("var_ready", at("var_ready", 1))
                    nc.gpsimd.tensor_tensor(rs1[:, p.t % RING], var2[:, :, :],
                                            mhalf[:, :].rearrange("p (a s) -> p a s", a=2), ALU.pow).then_inc(S["rstd_ready"], 1)
                if p.stage == "A2":
                    wait("xhat_ready", at("xhat_ready"))
                    nc.gpsimd.tensor_tensor(s_sb[:, :, :], x_sb[:, p.t % RING], rows_of(D), ALU.add).then_inc(S["pool_chain"], 1)
                    wait("y_ready", at("y_ready", 1))
                    nc.gpsimd.tensor_tensor(x1[:, :, :], x1[:, :, :], rows_of(0), ALU.add).then_inc(S["yb_ready"], 1)
                    wait("var_ready", at("var_ready", 1))
                    nc.gpsimd.tensor_tensor(rs[:, :], var2[:, 0], mhalf[:, 0:SUB], ALU.pow).then_inc(S["rstd_ready"], 1)
                    for u in range(2):
                        wait(f"pq_free{u}", at(f"pq_free{u}", 1))
                    wait("pool_chain", at("pool_chain", 1))
                    nc.gpsimd.tensor_tensor(s_sb[:, :, :], s_sb[:, :, :], x1[:, :, :], ALU.add).then_inc(S["s_ready"], 1)
                if p.stage == "C":
                    wait("var_ready", at("var_ready", 1))
                    nc.gpsimd.tensor_tensor(rs[:, :], var2[:, 0], mhalf[:, 0:SUB], ALU.pow).then_inc(S["rstd_ready"], 1)

            walk(pool, run)

        @block.scalar
        def _(act):
            wait = waiter(act)
            act.wait_ge(fold_done, 1)

            def run(p):
                at = p.at
                if p.stage == "D2":
                    for c in range(NC):
                        wait(f"pt_full{c}", at(f"pt_full{c}", 1))
                        nc.scalar.activation(xhT[:, c], pt[c][:, :], ACT.Identity).then_inc(S[f"pt_free{c}"], 1)
                    wait("acc_ready", at("acc_ready"))
                    for j in range(3 * NC):
                        wait(f"pq_full{j % 2}", at(f"pq_full{j % 2}", j // 2 + 1))
                        if j < 2 * NC:
                            wait("feat_ready", at("feat_ready", max(j - 1, 0)))
                            nc.scalar.activation(expb[:, j % 2], pq[j % 2][:, :], ACT.Exp,
                                                 bias=b_qkv[:, j:j + 1]).then_inc(S["exp_ready"], 1)
                        else:
                            if j == 2 * NC:
                                wait("v_out", at("v_out"))
                            dst = feat[:, 2, j % 2].rearrange("p (q j t g) -> p j q t g", q=NQ, j=2, t=TB)
                            src = pq[j % 2][:, :].rearrange("p (q t j g) -> p j q t g", q=NQ, j=2, t=TB)
                            for half in range(2):
                                last = nc.scalar.activation(dst[:, half], src[:, half], ACT.Identity,
                                                            bias=b_qkv[:, j:j + 1])
                            last.then_inc(S[f"pq_free{j % 2}"], 1)
                if p.stage == "B":
                    if isinstance(p.t, int) and p.t == 0:
                        act.wait_ge(const_done, 5)
                    for u in range(4):
                        wait(f"pt_full{u % 2}", at(f"pt_full{u % 2}", u // 2 + 1))
                        src = pt[u % 2][:, :].rearrange("p (g j e) -> p j g e", g=4, j=NQ)
                        dst = vb[:, :, :].rearrange("p (j g) e -> p j g e", j=NQ)[:, :, 4 * u:4 * u + 4]
                        for b in range(2):
                            last = nc.scalar.activation(dst[64 * b:64 * b + 64, :, :, 32 * b:32 * b + HD],
                                                        src[64 * b:64 * b + 64, :, :, 0:HD], ACT.Identity)
                        last.then_inc(S[f"pt_free{u % 2}"], 1)
                    wait("attnT_ready", at("attnT_ready"))
                    for r in range(ROUNDS):
                        wait(f"pq_full{r % 2}", at(f"pq_full{r % 2}", r // 2 + 1))
                        dst = ot[:, :, :].rearrange("p h (t g) -> p g h t", t=TB)[:, RG * r:RG * (r + 1)]
                        src = pq[r % 2][:, :].rearrange("p (g h t) -> p g h t", g=RG, h=H)
                        nc.scalar.activation(dst, src, ACT.Identity).then_inc(S[f"pq_free{r % 2}"], 1)
                if p.stage == "C":
                    for c in range(NC):
                        wait(f"pt_full{c}", at(f"pt_full{c}", 1))
                        nc.scalar.activation(hT[:, c], pt[c][:, :], ACT.Identity).then_inc(S[f"pt_free{c}"], 1)
                    for m in range(NM):
                        wait(f"pq_full{m % 2}", at(f"pq_full{m % 2}", m // 2 + 1))
                        nc.scalar.activation(hid[:, m], pq[m % 2][:, :], ACT.Gelu,
                                             bias=b_fc[:, m:m + 1]).then_inc(S[f"pq_free{m % 2}"], 1)
                if p.stage == "E":
                    for c in range(NC):
                        wait(f"pt_full{c}", at(f"pt_full{c}", 1))
                        nc.scalar.activation(zT[:, p.t % RING, c], pt[c][:, :], ACT.Identity,
                                             accum_out=pooled[:, c, bass.ds(p.t % RING, 1)]).then_inc(S[f"pt_free{c}"], 1)
                if p.stage == "G":
                    wait("logit_ready", at("logit_ready", 1))
                    nc.scalar.activation(g8[:, 3], g8[:, 2], ACT.Exp).then_inc(S["gexp_ready"], 1)
                if p.stage == "F":
                    wait("v_out", at("v_out"))
                    for j in range(2 * E):
                        wait(f"pq_full{j % 2}", at(f"pq_full{j % 2}", j // 2 + 1))
                        wait("acc_ready", at("acc_ready", max(j - 1, 0)))
                        nc.scalar.activation(ge[:, j % 2], pq[j % 2][:, :], ACT.Gelu,
                                             bias=b_e[:, j:j + 1]).then_inc(S[f"pq_free{j % 2}"], 1)

            walk(act, run)

        @block.vector
        def _(dve):
            wait = waiter(dve)
            dve.wait_ge(w_in[1], 16)
            dve.wait_ge(S["pt_full0"], 1)
            nc.vector.tensor_tensor(col[:, 8:8 + 3 * NC + NM], col[:, 8:8 + 3 * NC + NM],
                                    pt[0][:, 0:3 * NC + NM], ALU.add).then_inc(S["pt_free0"], 1)
            for n in range(3):
                for c in range(NC):
                    nc.vector.tensor_scalar(w_qkv[:, n, c], w_qkv[:, n, c], ln1w[:, c:c + 1], None, ALU.mult)
            for c in range(NC):
                last = nc.vector.tensor_scalar(w_fc[:, c], w_fc[:, c], ln2w[:, c:c + 1], None, ALU.mult)
            last.then_inc(fold_done, 1)
            dve.wait_ge(w_in[3], 16)
            dve.wait_ge(w_in[4], 16)
            dve.wait_ge(const_done, 5)

            def run(p):
                at = p.at
                links = [0]

                def link(ins):
                    links[0] += 1
                    ins.then_inc(S["dve_chain"], 1)
                    wait("dve_chain", at("dve_chain", links[0]))

                def transposed():
                    wait("pt_free0", at("pt_free0"))
                    wait("pt_free1", at("pt_free1"))

                def hold():
                    nc.vector.memset(held_at[:, :], 0.0)

                def stats(src, into):
                    hold()
                    for s in range(SUB):
                        last = nc.vector.bn_stats(stat[:, s], src[:, s])
                    link(last)
                    hold()
                    for s in range(SUB):
                        last = nc.vector.bn_aggr(into[:, s], stat[:, s])
                    link(last)

                def normed(dst, src, mean, rstd):
                    for s in range(SUB):
                        last = nc.vector.tensor_scalar(dst[:, s], src[:, s], mean(s), rstd(s), ALU.subtract, ALU.mult)
                    return last

                if p.stage in ("D1", "A2"):
                    slot = p.t % RING
                    m1 = mv1[:, slot]
                    r1 = rs1[:, slot]
                if p.stage == "D1":
                    wait("x_in", at("x_in"))
                    stats(x_sb[:, slot], mv)
                    nc.vector.tensor_copy(m1, mv[:, :, :])
                    nc.vector.tensor_scalar(var2[:, 0], mv[:, :, 1], 1.0 + EPS, EPS * EPS, ALU.mult, ALU.add)
                    nc.vector.tensor_scalar(var2[:, 1], mv[:, :, 1], EPS, None, ALU.add).then_inc(S["var_ready"], 1)
                    wait("rstd_ready", at("rstd_ready", 1))
                    transposed()
                    normed(xhat, x_sb[:, slot], lambda s: m1[:, s, 0:1], lambda s: r1[:, 0, s:s + 1]).then_inc(S["xhat_ready"], 1)
                if p.stage == "D2":
                    wait("out_stored", at("out_stored"))
                    for j in range(2 * NC):
                        if j % NC == 0:
                            c = "qk"[j // NC]
                            wait(f"{c}_out", at(f"{c}_out"))
                        wait("exp_ready", at("exp_ready", j + 1))
                        nc.vector.tensor_scalar(relub[:, j % 2], pq[j % 2][:, :], b_qkv[:, j:j + 1], 0.0,
                                                ALU.add, ALU.max).then_inc(S[f"pq_free{j % 2}"], 1)
                        wait(f"pq_free{j % 2}", at(f"pq_free{j % 2}", j // 2 + 1))
                        nc.vector.scalar_tensor_tensor(feat[:, j // NC, j % NC], expb[:, j % 2], 1.0, relub[:, j % 2],
                                                       ALU.min, ALU.add).then_inc(S["feat_ready"], 1)
                if p.stage == "B":
                    for r in range(ROUNDS):
                        if r >= 2:
                            wait(f"pq_full{r % 2}", at(f"pq_full{r % 2}", (r - 2) // 2 + 1))
                        for h in range(2):
                            wait(f"ps_full{r % 2}", at(f"ps_full{r % 2}", 2 * (r // 2) + h + 1))
                            nc.vector.tensor_tensor(am[:, r % 2, h].rearrange("p (g n) -> p g n", g=RG),
                                                    ps[r % 2][h][:, :].rearrange("p (g n) -> p g n", g=RG),
                                                    mask[:, :].unsqueeze(1).broadcast_to([P, RG, TB * H]),
                                                    ALU.mult).then_inc(S[f"ps_free{r % 2}"], 1)
                if p.stage == "A1":
                    wait("nd_in", at("nd_in"))
                    link(nc.vector.tensor_scalar(nd[:, 1], nd[:, 1], DEN_EPS, None, ALU.add))
                    link(nc.vector.reciprocal(nd[:, 1], nd[:, 1]))
                    nc.vector.tensor_tensor(attnT[:, :, :], nd[:, 0], nd[:, 1], ALU.mult).then_inc(S["attnT_ready"], 1)
                if p.stage == "A2":
                    wait("s_ready", at("s_ready"))
                    normed(x1, x_sb[:, slot], lambda s: m1[:, s, 0:1], lambda s: r1[:, 1, s:s + 1]).then_inc(S["y_ready"], 1)
                    wait("yb_ready", at("yb_ready", 1))
                    for u in range(2):
                        wait(f"pq_full{u}", at(f"pq_full{u}", 1))
                        o = x1[:, 2 * u:2 * u + 2].rearrange("p s d -> p (s d)")
                        nc.vector.tensor_tensor(o, o, pq[u][:, :], ALU.add).then_inc(S[f"pq_free{u}"], 1)
                    wait("pq_free1", at("pq_free1", 1))
                    stats(x1, mv)
                    nc.vector.tensor_scalar(var2[:, 0], mv[:, :, 1], EPS, None, ALU.add).then_inc(S["var_ready"], 1)
                    wait("rstd_ready", at("rstd_ready", 1))
                    transposed()
                    normed(hn, x1, lambda s: mv[:, s, 0:1], lambda s: rs[:, s:s + 1]).then_inc(S["h_ready"], 1)
                if p.stage == "C":
                    wait("s_ready", at("s_ready"))
                    x2 = x2_sb[:, p.t % RING]
                    for u in range(2):
                        wait(f"pq_full{u}", at(f"pq_full{u}", 5))
                        nc.vector.tensor_tensor(x2[:, 2 * u:2 * u + 2], pq[u][:, :].rearrange("p (s d) -> p s d", d=D),
                                                s_sb[:, 2 * u:2 * u + 2], ALU.add).then_inc(S[f"pq_free{u}"], 1)
                    wait("pq_free1", at("pq_free1", 5))
                    stats(x2, mv)
                    nc.vector.tensor_scalar(var2[:, 0], mv[:, :, 1], EPS, None, ALU.add).then_inc(S["var_ready"], 1)
                    wait("rstd_ready", at("rstd_ready", 1))
                    transposed()
                    normed(z, x2, lambda s: mv[:, s, 0:1], lambda s: rs[:, s:s + 1]).then_inc(S["z_ready"], 1)
                if p.stage == "G":
                    transposed()
                    link(nc.vector.reduce_sum(gs[:, 0:NC], pooled[:, :, :], AX))
                    for c in range(NC):
                        last = nc.vector.tensor_copy(pb128[:, c], gs[:, c:c + 1].broadcast_to([P, P]))
                    last.then_inc(S["pool_ready"], 1)
                    wait("pt_full0", at("pt_full0", 1))
                    link(nc.vector.scalar_tensor_tensor(g8[:, 0], pt[0][:, 0:E], 1.0 / SEQ, row[:, 2 * D:2 * D + E],
                                                        ALU.mult, ALU.add))
                    hold()
                    link(nc.vector.max(g8[:, 1], g8[:, 0]))
                    nc.vector.tensor_scalar(g8[:, 2], g8[:, 0], g8[:, 1, 0:1], None, ALU.subtract).then_inc(S["logit_ready"], 1)
                    link(nc.vector.tensor_scalar(g8[:, 4], g8[:, 0], g8[:, 1, 1:2], None, ALU.is_ge))
                    wait("gexp_ready", at("gexp_ready", 1))
                    link(nc.vector.tensor_tensor(g8[:, 3], g8[:, 3], g8[:, 4], ALU.mult))
                    link(nc.vector.reduce_sum(gs[:, 2:3], g8[:, 3], AX))
                    link(nc.vector.reciprocal(gs[:, 3:4], gs[:, 2:3]))
                    nc.vector.tensor_scalar(g8[:, 5], g8[:, 3], gs[:, 3:4], None, ALU.mult).then_inc(S["pt_free0"], 1)
                if p.stage == "F":
                    wait("pt_free0", at("pt_free0"))
                    wait("k_out", at("k_out"))
                    for j in range(2 * E):
                        e, m = j // 2, j % 2
                        wait(f"pq_free{m}", at(f"pq_free{m}", e + 1))
                        if e == 0:
                            ins = nc.vector.tensor_scalar(acc[:, m], ge[:, m], g8[:, 5, 0:1], None, ALU.mult)
                        else:
                            wait("acc_ready", at("acc_ready", j - 1))
                            ins = nc.vector.scalar_tensor_tensor(acc[:, m], ge[:, m], g8[:, 5, e:e + 1], acc[:, m],
                                                                 ALU.mult, ALU.add)
                        ins.then_inc(S["acc_ready"], 1)
                    wait("q_out", at("q_out"))
                    wait("out_stored", at("out_stored"))
                    for u in range(2):
                        wait(f"pt_full{u}", at(f"pt_full{u}", 1))
                        nc.vector.tensor_tensor(out_sb[:, 2 * u:2 * u + 2], pt[u][:, :].rearrange("p (s d) -> p s d", d=D),
                                                x2_sb[:, p.t % RING, 2 * u:2 * u + 2], ALU.add).then_inc(S[f"pt_free{u}"], 1)

            walk(dve, run)

        @block.tensor
        def _(pe):
            wait = waiter(pe)
            for n in (0, 1, 2, 5):
                pe.wait_ge(w_in[n], 16)
            for n in range(3 * NC + NM):
                for c in range(NC):
                    if n < 3 * NC:
                        w, b = w_qkv[:, n // NC, c, P * (n % NC):P * (n % NC + 1)], ln1b[:, c:c + 1]
                    else:
                        w, b = w_fc[:, c, P * (n - 3 * NC):P * (n - 3 * NC + 1)], ln2b[:, c:c + 1]
                    last = nc.tensor.matmul(pt[0][:, n:n + 1], w, b, start=(c == 0), stop=(c == NC - 1))
            last.then_inc(S["pt_full0"], 1)
            pe.wait_ge(fold_done, 1)
            for n in range(6, 10):
                pe.wait_ge(w_in[n], 16)

            def run(p):
                at = p.at

                def bank_q(n, k):
                    wait(f"pq_free{n}", at(f"pq_free{n}", k))

                def transposes(src):
                    for c in range(NC):
                        wait(f"pt_free{c}", at(f"pt_free{c}"))
                        for s in range(SUB):
                            last = nc.tensor.transpose(pt[c][:, P * s:P * (s + 1)], src[:, s, P * c:P * (c + 1)], ident[:, :])
                        last.then_inc(S[f"pt_full{c}"], 1)

                def copied(k):
                    for c in range(2):
                        wait(f"pt_free{c}", at(f"pt_free{c}", k))

                if p.stage == "D2":
                    wait("xhat_ready", at("xhat_ready"))
                    transposes(xhat)
                    copied(1)
                    for j in range(3 * NC):
                        bank_q(j % 2, j // 2)
                        for c in range(NC):
                            last = nc.tensor.matmul(pq[j % 2][:, :], w_qkv[:, j // NC, c, P * (j % NC):P * (j % NC + 1)],
                                                    xhT[:, c], start=(c == 0), stop=(c == NC - 1))
                        last.then_inc(S[f"pq_full{j % 2}"], 1)
                if p.stage == "B":
                    wait("v_in", at("v_in"))
                    for u in range(4):
                        wait(f"pt_free{u % 2}", at(f"pt_free{u % 2}", u // 2))
                        for g in range(4):
                            last = nc.tensor.transpose(pt[u % 2][:, P * g:P * (g + 1)],
                                                       vd[:, :, :, :].rearrange("p b h t -> p (b h t)")[:, 4 * u + g::GG // 2], ident[:, :])
                        last.then_inc(S[f"pt_full{u % 2}"], 1)
                    wait("q_in", at("q_in"))
                    wait("k_in", at("k_in"))

                    def weighted(r):
                        wait(f"ps_free{r % 2}", at(f"ps_free{r % 2}", 2 * (r // 2) + 2))
                        bank_q(r % 2, r // 2)
                        for g in range(RG):
                            for h in range(2):
                                last = nc.tensor.matmul(pq[r % 2][64 * h:64 * h + 64, 64 * g:64 * g + 64],
                                                        vb[:, GG * h + RG * r + g], am[:, r % 2, h, 64 * g:64 * g + 64],
                                                        start=True, stop=True)
                        last.then_inc(S[f"pq_full{r % 2}"], 1)

                    def block_of(src, q, gg):
                        return src[q:q + HD].rearrange("d h t -> d (h t)")[:, gg::GG]

                    for r in range(ROUNDS):
                        wait(f"ps_free{r % 2}", at(f"ps_free{r % 2}", 2 * (r // 2)))
                        for h in range(2):
                            for g in range(RG):
                                gg = RG * r + g
                                for b in range(2):
                                    q = 32 * (2 * h + b)
                                    last = nc.tensor.matmul(ps[r % 2][h][64 * b:64 * b + 64, 64 * g:64 * g + 64],
                                                            block_of(kd, q, gg), block_of(qd, q, gg),
                                                            start=True, stop=True)
                            last.then_inc(S[f"ps_full{r % 2}"], 1)
                        if r == 1:
                            copied(2)
                        if r >= 1:
                            weighted(r - 1)
                    weighted(ROUNDS - 1)
                if p.stage == "A2":
                    wait("attnT_ready", at("attnT_ready"))
                    for u in range(2):
                        bank_q(u, 0)
                        for s in range(2):
                            for c in range(NC):
                                lo = P * (2 * u + s)
                                last = nc.tensor.matmul(pq[u][:, D * s:D * (s + 1)], attnT[:, c, lo:lo + P], w_o[:, c],
                                                        start=(c == 0), stop=(c == NC - 1))
                        last.then_inc(S[f"pq_full{u}"], 1)
                if p.stage == "C":
                    wait("h_ready", at("h_ready"))
                    transposes(hn)
                    copied(1)
                    for m in range(NM):
                        bank_q(m % 2, m // 2)
                        for c in range(NC):
                            last = nc.tensor.matmul(pq[m % 2][:, :], w_fc[:, c, P * m:P * (m + 1)], hT[:, c],
                                                    start=(c == 0), stop=(c == NC - 1))
                        last.then_inc(S[f"pq_full{m % 2}"], 1)
                    bank_q(0, NM // 2)
                    bank_q(1, NM // 2)
                    for u in range(2):
                        bank_q(u, 4)
                        for s in range(2):
                            for m in range(NM):
                                lo = P * (2 * u + s)
                                last = nc.tensor.matmul(pq[u][:, D * s:D * (s + 1)], hid[:, m, lo:lo + P], w_pj[:, m],
                                                        start=(m == 0), stop=(m == NM - 1))
                        last.then_inc(S[f"pq_full{u}"], 1)
                if p.stage == "E":
                    wait("z_ready", at("z_ready"))
                    transposes(z)
                if p.stage == "G":
                    wait("pool_ready", at("pool_ready", 1))
                    wait("pt_free0", at("pt_free0"))
                    for c in range(NC):
                        last = nc.tensor.matmul(pt[0][:, 0:E], pb128[:, c], w_g[:, c], start=(c == 0), stop=(c == NC - 1))
                    last.then_inc(S["pt_full0"], 1)
                if p.stage == "F":
                    copied(0)
                    for j in range(2 * E):
                        e, m = j // 2, j % 2
                        bank_q(m, e)
                        for c in range(NC):
                            last = nc.tensor.matmul(pq[m][:, :], w_e[:, e, c, P * m:P * (m + 1)], zT[:, p.t % RING, c],
                                                    start=(c == 0), stop=(c == NC - 1))
                        last.then_inc(S[f"pq_full{m}"], 1)
                    wait("acc_ready", at("acc_ready", 2 * E))
                    for u in range(2):
                        wait(f"pt_free{u}", at(f"pt_free{u}"))
                        for s in range(2):
                            for m in range(NC):
                                lo = P * (2 * u + s)
                                last = nc.tensor.transpose(pt[u][:, D * s + P * m:D * s + P * (m + 1)],
                                                           acc[:, m, lo:lo + P], ident[:, :])
                        last.then_inc(S[f"pt_full{u}"], 1)

            walk(pe, run)


def kernel(**inputs):
    import concourse.bacc as bacc
    from concourse.bass_utils import run_bass_kernel_spmd

    get = {k.replace("L0_", ""): np.asarray(v) for k, v in inputs.items()}

    def chunks(w):
        return np.moveaxis(w.reshape(-1, P, *w.shape[1:]), 1, 0)

    arrays = {
        "x": get["attn_q_x"].reshape(BATCH * SEQ, D),
        "wqkv": np.stack([chunks(get["attn_w" + n]) for n in "qkv"], 1),
        "wo": chunks(get["attn_wo"]),
        "fcw": chunks(get["attn_fc_w"]),
        "pjw": chunks(get["attn_proj_w"]),
        "gw": chunks(get["ffn_gate_w"].T),
        "ew": np.stack([chunks(w.T) for w in get["ffn_expert_w"]], 1),
        "cols": np.concatenate([chunks(get[n]) for n in (
            "attn_ln1_w", "attn_ln1_b", "attn_ln2_w", "attn_ln2_b", "attn_bq", "attn_bk", "attn_bv", "attn_fc_b")]
            + [chunks(b) for b in get["ffn_expert_b"]], 1),
        "rows": np.tile(np.concatenate([get["attn_bo"], get["attn_proj_b"], get["ffn_gate_b"]])[None], (P, 1)),
        "ident": np.eye(P, dtype=np.float32),
        "mask": (np.arange(P)[:, None] % TB == np.arange(TB * H)[None] % TB).astype(np.float32),
    }
    nc = bacc.Bacc("TRN2", target_bir_lowering=False, num_devices=1)
    maps, args = {}, []
    for name, a in arrays.items():
        a = np.ascontiguousarray(a)
        maps[f"in_{name}"] = a
        args.append(nc.dram_tensor(f"in_{name}", a.shape, mybir.dt.from_np(a.dtype), kind="ExternalInput").ap())
    out = nc.dram_tensor("out", (BATCH * SEQ, D), mybir.dt.float32, kind="ExternalOutput").ap()
    build(nc, *args, out)
    r = run_bass_kernel_spmd(nc, [maps], core_ids=[0])
    return r.results[0]["out"].reshape(BATCH, SEQ, D)
```

```python
import numpy as np
from contextlib import ExitStack

import concourse.bass as bass
from concourse import mybir

BATCH, SEQ, D = 4, 2048, 256
H, HD = 16, 16
MLP = 4 * D
E = 8
TOP = 2
P = 128
NC = D // P
NM = MLP // P
T = 512
SUB = T // P
TILES = BATCH * SEQ // T
PER_BATCH = SEQ // T
RING = 4
NQ = 4
QT = T // NQ
TB = 4
GG = QT // TB
RG = 8
ROUNDS = GG // RG
K_PARTS, Q_PARTS = (0, 1, 0), (0, 0, 1)
KP = HD * len(K_PARTS)
TERMS = tuple(zip(K_PARTS, Q_PARTS))
EPS = 1e-5
DEN_EPS = 1e-6

LAG = {"L": 0, "D1": 0, "X": 0, "D2": 0, "QK": 0, "VT": 0, "B": 1, "A1": 1, "N": 1, "Y": 1, "A2": 1,
       "R": 2, "H": 2, "C1": 2, "C2": 2, "J": 2, "E": 2, "F1": 6, "F2": 6}
FULL = ["L", "F1", "B", "R", "F2", "D1", "H", "C1", "X", "C2", "A1", "D2", "N", "Y", "J", "QK", "A2", "VT", "E"]

INC = {
    "pt_full0": {"P": 1, "X": 1, "VT": 2, "H": 1, "E": 1, "F2": 1, "G": 1},
    "pt_free0": {"P": 1, "X": 1, "VT": 2, "H": 1, "E": 1, "F2": 1, "G": 1},
    "pt_full1": {"X": 1, "VT": 2, "H": 1, "E": 1, "F2": 1},
    "pt_free1": {"X": 1, "VT": 2, "H": 1, "E": 1, "F2": 1},
    "pq_full0": {"D2": 2, "B": 4, "C1": 2, "C2": 2, "F1": TOP},
    "pq_free0": {"D2": 2, "B": 4, "C1": 2, "C2": 2, "F1": TOP},
    "pq_full1": {"D2": 2, "B": 4, "C1": 2, "C2": 2, "F1": TOP},
    "pq_free1": {"D2": 2, "B": 4, "C1": 2, "C2": 2, "F1": TOP},
    "am_used": {"B": 8},
    "ps_full0": {"B": 8, "J": 2}, "ps_free0": {"B": 8, "J": 2},
    "ps_full1": {"B": 8, "A2": 2, "D2": 2}, "ps_free1": {"B": 8, "A2": 2, "D2": 2},
    "x_in": {"L": 16},
    "var_ready": {"D1": 1, "A2": 1, "J": 1},
    "rstd_ready": {"D1": 1, "A2": 1, "J": 1},
    "xhat_ready": {"D1": 1},
    "feat_ready": {"D2": 12},
    "q_out": {"D2": 32}, "k_out": {"D2": 32}, "v_out": {"D2": 16},
    "q_in": {"QK": 96}, "k_in": {"QK": 96}, "v_in": {"D2": 128},
    "nd_out": {"B": 128}, "num_in": {"B": 16}, "den_in": {"B": 16},
    "rden_ready": {"A1": 1}, "rden_out": {"A1": 16}, "rden_in": {"A1": 16 * P // H},
    "attnT_ready": {"N": 1},
    "y_ready": {"Y": 1}, "yb_ready": {"Y": 1}, "s_ready": {"P": 1, "A2": 1},
    "h_ready": {"R": 1}, "rest_ready": {"C1": NM // 2, "C2": NM // 2},
    "z_ready": {"J": 1},
    "pool_ready": {"G": 1}, "logit_ready": {"G": 1}, "gexp_ready": {"G": 1},
    "acc_ready": {"P": 1, "F1": 2 * TOP},
    "out_stored": {"P": 16, "F2": 16},
    "dve_chain": {"D1": 2, "A1": 1, "A2": 2, "J": 2, "G": 13},
    "xw_in": {"P": 16, "F1": 32 * E}, "x_mm": {"P": 1, "F1": 2 * E}, "x_ge": {"P": 1, "F1": 2 * E},
    "x_sum": {"P": 1, "F1": 2 * E},
    "choice_ready": {"G": 1}, "chosen_in": {"P": 16, "G": 64},
    "pool_chain": {"Y": 1},
}


class Place:

    def __init__(self, stage, i, base, rates):
        self.stage, self.i, self.base, self.rates = stage, i, base, rates
        self.t = i - LAG[stage] if stage in LAG else None

    def at(self, name, more=0):
        value = self.base.get(name, 0) + more
        for index, rate in self.rates:
            if rate.get(name, 0):
                value = index * rate[name] + value
        return value


def total(stages):
    out = {}
    for name, by in INC.items():
        out[name] = sum(by.get(s, 0) for s in stages)
    return out


def plus(a, b, times=1):
    return {k: a.get(k, 0) + times * b.get(k, 0) for k in INC}


def walk(eng, run):
    base = total(["P"])

    def stages(names, i, rates):
        nonlocal base
        for s in names:
            run(Place(s, i, base, rates))
            base = plus(base, total([s]))

    def loop(lo, hi, names):
        nonlocal base
        rate = total(names)
        at = base
        with eng.Fori(0, hi - lo) as k:
            stages(names, k + lo, [(k, rate)])
        base = plus(at, rate, hi - lo)

    def drop(*out):
        return [s for s in FULL if s not in out]

    stages(["L", "D1", "X", "D2", "QK", "VT"], 0, [])
    stages(drop("F1", "F2", "R", "H", "C1", "C2", "J", "E"), 1, [])
    stages(drop("F1", "F2"), 2, [])
    loop(3, 6, drop("F1", "F2"))
    at, rate, epoch = base, total(FULL), plus(total(["G"]), total(FULL), PER_BATCH)
    with eng.Fori(0, 2) as e:
        stages(["G"], 0, [(e, epoch)])
        with eng.Fori(0, PER_BATCH) as k:
            stages(FULL, e * PER_BATCH + k + 6, [(e, epoch), (k, rate)])
    base = plus(at, epoch, 2)
    stages(["G"], 0, [])
    loop(14, 16, FULL)
    stages(drop("L", "D1", "X", "D2", "QK", "VT"), 16, [])
    stages(["F1", "R", "F2", "H", "C1", "C2", "J", "E"], 17, [])
    stages(["G"], 0, [])
    loop(18, 22, ["F1", "F2"])


def build(nc, x, wqkv, wo, fcw, pjw, gw, ew, eb, cols, rows, ident_d, mask_d, out):
    f32 = mybir.dt.float32
    f32r = mybir.dt.float32r
    ALU = mybir.AluOpType
    ACT = mybir.ActivationFunctionType
    AX = mybir.AxisListType.X

    ctx = ExitStack()
    with ctx:
        def sb(name, shape, dt=f32):
            return ctx.enter_context(nc.sbuf_tensor(name, shape, dt))

        def sem(name):
            return ctx.enter_context(nc.semaphore(name))

        w_qkv = sb("w_qkv", [P, 3, NC, D])
        w_o = sb("w_o", [P, NC, D])
        w_fc = sb("w_fc", [P, NC, MLP])
        w_pj = sb("w_pj", [P, 2, NM, D], f32r)
        w_g = sb("w_g", [P, NC, E])
        w_e = sb("w_e", [P, TOP, NC, D])
        b_e = sb("b_e", [P, TOP + 1, NC])
        NCOL = 4 * NC + 3 * NC + NM
        col = sb("col", [P, NCOL])
        ln1w, ln1b, ln2w, ln2b = (col[:, NC * n:NC * (n + 1)] for n in range(4))
        b_qkv = col[:, 8:8 + 3 * NC]
        b_fc = col[:, 8 + 3 * NC:8 + 3 * NC + NM]
        row = sb("row", [P, 2 * D + 2 * E])
        ident = sb("ident", [P, P])
        mask = sb("mask", [P, P])
        mhalf = sb("mhalf", [P, 2 * SUB])
        x_sb = sb("x_sb", [P, RING, SUB, D])
        x2_sb = sb("x2_sb", [P, RING, SUB, D])
        w_pj32 = x2_sb[:, :, :, :].rearrange("p r s d -> p (r s) d")[:, 0:NM]
        zT = sb("zT", [P, RING, NC, T])
        pooled = sb("pooled", [P, NC, RING])
        mv1 = sb("mv1", [P, RING, SUB, 2])
        rs1 = sb("rs1", [P, RING, 2, SUB])
        stat = sb("stat", [P, SUB, 6])
        mv = sb("mv", [P, SUB, 2])
        var2 = sb("var2", [P, 2, SUB])
        rs = sb("rs", [P, SUB])
        xhat = sb("xhat", [P, SUB, D])
        hn = sb("hn", [P, SUB, D])
        z = hn
        xhT = sb("xhT", [P, NC, T])
        hT = sb("hT", [P, NC, T])
        feat = sb("feat", [P, 2, NC, 2, T], f32r)
        feat_v = sb("feat_v", [P, NC, T])
        out_sb = feat[:, 0, 0].bitcast(f32).rearrange("p c t -> p (c t)").rearrange("p (s d) -> p s d", d=D)
        acc = feat[:, 1, 0].bitcast(f32)
        ge = feat_v
        hid = sb("hid", [P, 2, NM * T], f32r)
        hidden = hid[:, :, :].rearrange("p w (m t) -> p w m t", t=T)
        qd, kd = hid[:, 0], hid[:, 1]
        vd = sb("vd", [P, 2, H, QT // 2])
        vb = sb("vb", [P, 2 * GG, 2 * HD])
        am = sb("am", [P, 4, 512])
        expb, relub = am[:, 0:2], am[:, 2:4]
        gelub = am[:, 0:2]
        ot = sb("ot", [P, 2, H, QT])
        nd = ot[:, :, :, :].rearrange("p b h t -> p (b h t)").rearrange("p (n t) -> p n t", t=T)
        num, rden = nd[:, 0:NC], nd[:, NC]
        den = sb("den", [P, H * T // P])
        attnT = sb("attnT", [P, NC, T])
        w_x = attnT[:, :, :].rearrange("p c t -> p (c t)")[:, 0:NC * D].rearrange("p (c d) -> p c d", d=D)
        x1 = xhat
        pb128 = sb("pb128", [P, NC, P])
        held_at = sb("held_at", [P, 1])
        held_act = sb("held_act", [P, 2])
        g8 = sb("g8", [P, 11, E])
        LOGIT, TOP8, SHIFTED, EXP, CHOSEN, GATE, RANK, RANK8, REST, ONE = range(10)
        gs = sb("gs", [P, 4])
        gtop = sb("gtop", [P, TOP])
        choice = sb("choice", [P, 4])
        choice_i = ctx.enter_context(nc.sbuf_tensor("choice_i", [P, 4], mybir.dt.int32))

        pt = [ctx.enter_context(nc.psum_tensor(f"pt{n}", [P, 512], f32)) for n in range(2)]
        pq = [ctx.enter_context(nc.psum_tensor(f"pq{n}", [P, 512], f32)) for n in range(2)]
        ps = [[ctx.enter_context(nc.psum_tensor(f"ps{n}{p}", [P, 512], f32)) for p in range(2)] for n in range(2)]

        qk_dram = [nc.dram_tensor(f"scratch_{n}", (2, NQ, D, QT), f32, kind="Internal").ap() for n in "qk"]
        v_dram = nc.dram_tensor("scratch_v", (D, T), f32, kind="Internal").ap()
        num_dram = nc.dram_tensor("scratch_num", (D, T), f32, kind="Internal").ap()
        den_dram = nc.dram_tensor("scratch_den", (H, T), f32, kind="Internal").ap()
        rden_dram = nc.dram_tensor("scratch_rden", (H, T), f32, kind="Internal").ap()

        S = {name: sem(name) for name in INC}
        w_in = [sem(f"w_in{n}") for n in range(9)]
        fold_done = sem("fold_done")
        const_done = sem("const_done")
        split_done = sem("split_done")

        x_t = x.rearrange("(n s p) d -> n p s d", s=SUB, p=P)
        out_t = out.rearrange("(n s p) d -> n p s d", s=SUB, p=P)

        block = ctx.enter_context(nc.Block())

        held = sem("held")

        def waiter(eng, own=False):
            def wait(name, value):
                if not isinstance(value, int) or value > 0:
                    eng.wait_ge(S[name], value)
                    if own and not isinstance(value, int):
                        eng.sem_inc(held, 1)
            return wait

        def qk_bank(j):
            if j < NC:
                return ps[1][j], "ps_full1", j + 1
            return pq[j - NC], f"pq_full{j - NC}", 2

        def hidden_chunks(p):
            return ((m, m + (NM // 2 if p.stage == "C2" else 0)) for m in range(NM // 2))

        def more_chosen(eng):
            return eng.value_load(choice_i[0:1, TOP:TOP + 1], min_val=0, max_val=1)

        @block.sync
        def _(sp):
            wait = waiter(sp, own=True)
            for n, (dst, src) in enumerate([
                (ident[:, :], ident_d), (col[:, :], cols), (w_qkv[:, :, :, :], wqkv), (row[:, :], rows),
                (mask[:, :], mask_d), (w_fc[:, :, :], fcw), (w_o[:, :, :], wo), (w_pj32, pjw),
                (w_g[:, :, :], gw),
            ]):
                sp.dma_start(dst, src).then_inc(w_in[n], 16)

            def run(p):
                at = p.at
                if p.stage == "L":
                    wait("xhat_ready", at("xhat_ready"))
                    sp.dma_start(x_sb[:, p.t % RING], x_t[p.t]).then_inc(S["x_in"], 16)
                if p.stage == "D2":
                    wait("v_in", at("v_in"))
                    for b in range(2):
                        wait(f"pq_free{b}", at(f"pq_free{b}", 1))
                    sp.dma_start(v_dram.rearrange("(c p) t -> p c t", p=P), feat_v[:, :, :]).then_inc(S["v_out"], 16)
                    for n, c in enumerate("qk"):
                        wait(f"{c}_in", at(f"{c}_in"))
                        for m in range(NC):
                            wait("feat_ready", at("feat_ready", 3 * (NC * n + m + 1)))
                            sp.dma_start(qk_dram[n].rearrange("w q (c p) t -> c p (w q) t", p=P)[m],
                                         feat[:, n, m].bitcast(f32).rearrange("p w (q t) -> p (w q) t", t=QT)
                                         ).then_inc(S[f"{c}_out"], 16)
                        if n == 0:
                            wait("v_out", at("v_out", 16))
                            if isinstance(p.t, int) and p.t == 0:
                                sp.wait_ge(const_done, 4)
                            for j in range(NQ):
                                src = v_dram.rearrange("(h d) (p b j t) -> p j b d h t", d=HD, p=2, b=2, j=2)
                                for b in range(2):
                                    sp.dma_start(vd[32 * j:32 * j + HD, b], src[j // 2, j % 2, b]).then_inc(S["v_in"], 16)
                if p.stage == "QK":
                    wait("ps_full0", at("ps_full0"))
                    wait("ps_full1", at("ps_full1"))
                    for n, (c, dst, parts) in enumerate((("q", qd, Q_PARTS), ("k", kd, K_PARTS))):
                        wait(f"{c}_out", at(f"{c}_out"))
                        for hf in range(2):
                            for r, w in enumerate(parts):
                                lo = 64 * hf + HD * r
                                sp.dma_start(dst[lo:lo + HD].bitcast(f32).rearrange("d (a t) -> d a t", t=QT),
                                             qk_dram[n][w, 2 * hf:2 * hf + 2].rearrange("b (h d) t -> d (b h) t", d=HD)
                                             ).then_inc(S[f"{c}_in"], 16)
                if p.stage == "B":
                    for b in range(2):
                        wait(f"pq_free{b}", at(f"pq_free{b}", ROUNDS))
                    for q in range(NQ):
                        ts = slice(QT * q, QT * (q + 1))
                        sp.dma_start(den_dram.rearrange("(o h) t -> o h t", o=1)[:, :, ts],
                                     ot[32 * (q // 2) + HD:32 * (q // 2) + HD + 1, q % 2]).then_inc(S["nd_out"], 16)
                        sp.dma_start(num_dram.rearrange("(e h) t -> e h t", h=H)[:, :, ts],
                                     ot[32 * (q // 2):32 * (q // 2) + HD, q % 2]).then_inc(S["nd_out"], 16)
                    wait("nd_out", at("nd_out", 128))
                    sp.dma_start(den[:, :], den_dram.rearrange("h (a b) -> (h a) b", b=H * T // P)).then_inc(S["den_in"], 16)
                    sp.dma_start(num, num_dram.rearrange("(c p) t -> p c t", p=P)).then_inc(S["num_in"], 16)
                if p.stage == "A1":
                    wait("rden_ready", at("rden_ready", 1))
                    sp.dma_start(rden_dram.rearrange("h (a b) -> (h a) b", b=H * T // P), den[:, :]).then_inc(S["rden_out"], 16)
                    wait("rden_out", at("rden_out", 16))
                    for e in range(P // H):
                        sp.dma_start(rden[H * e:H * (e + 1)], rden_dram).then_inc(S["rden_in"], 16)
                if p.stage == "F1":
                    wait("ps_full1", at("ps_full1"))
                    wait("choice_ready", at("choice_ready"))
                    more = more_chosen(sp)
                    with sp.If(more > 0):
                        with sp.Fori(0, E) as e:
                            sp.wait_ge(S["x_sum"], at("x_sum", 2 * e))
                            sp.sem_inc(held, 1)
                            sp.dma_start(w_x, ew[:, e]).then_inc(S["xw_in"], 16)
                            sp.dma_start(b_e[:, TOP], eb[:, e]).then_inc(S["xw_in"], 16)
                    with sp.Else():
                        sp.sem_inc(S["xw_in"], 32 * E)
                if p.stage == "F2":
                    for u in range(2):
                        wait(f"pt_free{u}", at(f"pt_free{u}", 1))
                    sp.dma_start(out_t[p.t], out_sb).then_inc(S["out_stored"], 16)

            walk(sp, run)
            sp.wait_ge(S["out_stored"], 16 * (TILES + 1))

        @block.gpsimd
        def _(pool):
            wait = waiter(pool)
            nc.gpsimd.memset(mhalf[:, :], -0.5).then_inc(const_done, 1)
            nc.gpsimd.memset(vd[:, :, :, :], 0.0).then_inc(const_done, 1)
            nc.gpsimd.memset(vb[:, :, :], 1.0).then_inc(const_done, 1)
            nc.gpsimd.memset(held_act[:, :], 0.0).then_inc(const_done, 1)
            pool.wait_ge(w_in[3], 16)

            pool.sem_inc(S["s_ready"], 1)
            pool.sem_inc(S["acc_ready"], 1)
            pool.sem_inc(S["out_stored"], 16)
            for name in ("x_mm", "x_ge", "x_sum"):
                pool.sem_inc(S[name], 1)
            pool.sem_inc(S["xw_in"], 16)
            pool.sem_inc(S["chosen_in"], 16)

            def rows_of(lo):
                return row[:, lo:lo + D].unsqueeze(1).broadcast_to([P, SUB, D])

            def run(p):
                at = p.at
                if p.stage == "D1":
                    wait("var_ready", at("var_ready", 1))
                    nc.gpsimd.tensor_tensor(rs1[:, p.t % RING], var2[:, :, :],
                                            mhalf[:, :].rearrange("p (a s) -> p a s", a=2), ALU.pow).then_inc(S["rstd_ready"], 1)
                if p.stage == "Y":
                    wait("y_ready", at("y_ready", 1))
                    nc.gpsimd.tensor_tensor(x1[:, :, :], x1[:, :, :], rows_of(0), ALU.add).then_inc(S["yb_ready"], 1)
                    slot = x_sb[:, p.t % RING]
                    nc.gpsimd.tensor_tensor(slot, slot, rows_of(D), ALU.add).then_inc(S["pool_chain"], 1)
                if p.stage == "A2":
                    slot = x_sb[:, p.t % RING]
                    wait("var_ready", at("var_ready", 1))
                    nc.gpsimd.tensor_tensor(rs[:, :], var2[:, 0], mhalf[:, 0:SUB], ALU.pow).then_inc(S["rstd_ready"], 1)
                    wait("ps_free1", at("ps_free1", 2))
                    wait("pool_chain", at("pool_chain"))
                    pool.sem_inc(held, 1)
                    nc.gpsimd.tensor_tensor(slot, slot, x1[:, :, :], ALU.add).then_inc(S["s_ready"], 1)
                if p.stage == "J":
                    wait("var_ready", at("var_ready", 1))
                    nc.gpsimd.tensor_tensor(rs[:, :], var2[:, 0], mhalf[:, 0:SUB], ALU.pow).then_inc(S["rstd_ready"], 1)

            walk(pool, run)

        @block.scalar
        def _(act):
            wait = waiter(act)
            act.wait_ge(fold_done, 1)
            act.wait_ge(const_done, 4)

            def run(p):
                at = p.at
                if p.stage == "X":
                    for c in range(NC):
                        wait(f"pt_full{c}", at(f"pt_full{c}", 1))
                        nc.scalar.activation(xhT[:, c], pt[c][:, :], ACT.Identity).then_inc(S[f"pt_free{c}"], 1)
                if p.stage == "D2":
                    nc.scalar.activation(held_act[:, 1:2], held_act[:, 0:1], ACT.Exp)
                    wait("acc_ready", at("acc_ready"))
                    wait("v_out", at("v_out"))
                    for m in range(NC):
                        wait(f"pq_full{m}", at(f"pq_full{m}", 1))
                        dst = feat_v[:, m].rearrange("p (q j t g) -> p j q t g", q=NQ, j=2, t=TB)
                        src = pq[m][:, :].rearrange("p (q t j g) -> p j q t g", q=NQ, j=2, t=TB)
                        for half in range(2):
                            last = nc.scalar.activation(dst[:, half], src[:, half], ACT.Identity,
                                                        bias=b_qkv[:, 2 * NC + m:2 * NC + m + 1])
                        last.then_inc(S[f"pq_free{m}"], 1)
                    wait("rest_ready", at("rest_ready"))
                    for j in range(2 * NC):
                        bank, full, k = qk_bank(j)
                        wait(full, at(full, k))
                        wait("feat_ready", at("feat_ready", 3 * max(j - 1, 0)))
                        nc.scalar.activation(expb[:, j % 2], bank[:, :], ACT.Exp, bias=b_qkv[:, j:j + 1])
                        nc.scalar.activation(relub[:, j % 2], bank[:, :], ACT.Relu,
                                             bias=b_qkv[:, j:j + 1]).then_inc(S[full.replace("full", "free")], 1)
                if p.stage == "VT":
                    for u in range(4):
                        wait(f"pt_full{u % 2}", at(f"pt_full{u % 2}", u // 2 + 1))
                        src = pt[u % 2][:, :].rearrange("p (g j e) -> p j g e", g=4, j=NQ)[:, :, :, 0:HD]
                        dst = vb[:, :, :].rearrange("p (j g) e -> p j g e", j=NQ)[:, :, 4 * u:4 * u + 4, 0:HD]
                        nc.scalar.activation(dst, src, ACT.Identity).then_inc(S[f"pt_free{u % 2}"], 1)
                if p.stage == "B":
                    wait("attnT_ready", at("attnT_ready"))
                    rows = slice(0, 64)
                    for r in range(ROUNDS):
                        for u in range(2):
                            wait(f"pq_full{u}", at(f"pq_full{u}", r + 1))
                            dst = ot[rows].rearrange("p b h (t g) -> p g (b h) t", t=TB)
                            src = pq[u][rows, :].rearrange("p (g a t) -> p g a t", g=RG // 2, t=TB)
                            lo = RG * r + RG // 2 * u
                            nc.scalar.activation(dst[:, lo:lo + RG // 2], src, ACT.Identity).then_inc(S[f"pq_free{u}"], 1)
                if p.stage == "H":
                    for c in range(NC):
                        wait(f"pt_full{c}", at(f"pt_full{c}", 1))
                        nc.scalar.activation(hT[:, c], pt[c][:, :], ACT.Identity).then_inc(S[f"pt_free{c}"], 1)
                if p.stage in ("C1", "C2"):
                    for k, m in hidden_chunks(p):
                        wait(f"pq_full{m % 2}", at(f"pq_full{m % 2}", k // 2 + 1))
                        wait("rest_ready", at("rest_ready", k - 1 if p.stage == "C2" else max(k - 1, 0)))
                        nc.scalar.activation(gelub[:, m % 2], pq[m % 2][:, :], ACT.Gelu, bias=b_fc[:, m:m + 1])
                        nc.scalar.activation(hidden[:, 0, m], pq[m % 2][:, :], ACT.Gelu,
                                             bias=b_fc[:, m:m + 1]).then_inc(S[f"pq_free{m % 2}"], 1)
                if p.stage == "E":
                    for c in range(NC):
                        wait(f"pt_full{c}", at(f"pt_full{c}", 1))
                        nc.scalar.activation(zT[:, p.t % RING, c], pt[c][:, :], ACT.Identity,
                                             accum_out=pooled[:, c, bass.ds(p.t % RING, 1)]).then_inc(S[f"pt_free{c}"], 1)
                if p.stage == "G":
                    wait("logit_ready", at("logit_ready", 1))
                    nc.scalar.activation(g8[:, EXP], g8[:, SHIFTED], ACT.Exp).then_inc(S["gexp_ready"], 1)
                    wait("acc_ready", at("acc_ready"))
                    wait("x_sum", at("x_sum"))
                    wait("choice_ready", at("choice_ready", 1))
                    act.sem_inc(held, 1)
                    for n in range(TOP):
                        e = act.value_load(choice_i[0:1, n:n + 1], min_val=0, max_val=E - 1)
                        act.dma_start(w_e[:, n], ew[:, e]).then_inc(S["chosen_in"], 16)
                        act.dma_start(b_e[:, n], eb[:, e]).then_inc(S["chosen_in"], 16)
                if p.stage == "F1":
                    nc.scalar.activation(held_act[:, 1:2], held_act[:, 0:1], ACT.Gelu)
                    wait("v_out", at("v_out"))
                    wait("chosen_in", at("chosen_in"))
                    for e in range(TOP):
                        for m in range(NC):
                            wait(f"pq_full{m}", at(f"pq_full{m}", e + 1))
                            wait("acc_ready", at("acc_ready", max(2 * e + m - 1, 0)))
                            nc.scalar.activation(ge[:, m], pq[m][:, :], ACT.Gelu,
                                                 bias=b_e[:, e, m:m + 1]).then_inc(S[f"pq_free{m}"], 1)
                    more = more_chosen(act)
                    with act.If(more > 0):
                        wait("acc_ready", at("acc_ready", 2 * TOP))
                        with act.Fori(0, E) as e:
                            for m in range(NC):
                                act.wait_ge(S["x_mm"], at("x_mm", 2 * e + m + 1))
                                nc.scalar.activation(ge[:, m], pq[m][:, :], ACT.Gelu,
                                                     bias=b_e[:, TOP, m:m + 1]).then_inc(S["x_ge"], 1)
                    with act.Else():
                        act.sem_inc(S["x_ge"], 2 * E)

            walk(act, run)

        @block.vector
        def _(dve):
            wait = waiter(dve)
            dve.wait_ge(w_in[1], 16)
            dve.wait_ge(S["pt_full0"], 1)
            nc.vector.tensor_tensor(col[:, 8:8 + 3 * NC + NM], col[:, 8:8 + 3 * NC + NM],
                                    pt[0][:, 0:3 * NC + NM], ALU.add).then_inc(S["pt_free0"], 1)
            for n in range(3):
                for c in range(NC):
                    nc.vector.tensor_scalar(w_qkv[:, n, c], w_qkv[:, n, c], ln1w[:, c:c + 1], None, ALU.mult)
            for c in range(NC):
                last = nc.vector.tensor_scalar(w_fc[:, c], w_fc[:, c], ln2w[:, c:c + 1], None, ALU.mult)
            last.then_inc(fold_done, 1)
            dve.wait_ge(w_in[3], 16)
            dve.wait_ge(w_in[4], 16)
            dve.wait_ge(const_done, 4)

            def run(p):
                at = p.at
                links = [0]

                def link(ins):
                    links[0] += 1
                    ins.then_inc(S["dve_chain"], 1)
                    wait("dve_chain", at("dve_chain", links[0]))

                def transposed():
                    wait("pt_free0", at("pt_free0"))
                    wait("pt_free1", at("pt_free1"))

                def hold():
                    nc.vector.memset(held_at[:, :], 0.0)

                def stats(src, into):
                    hold()
                    for s in range(SUB):
                        last = nc.vector.bn_stats(stat[:, s], src[:, s])
                    link(last)
                    hold()
                    for s in range(SUB):
                        last = nc.vector.bn_aggr(into[:, s], stat[:, s])
                    link(last)

                def normed(dst, src, mean, rstd):
                    for s in range(SUB):
                        last = nc.vector.tensor_scalar(dst[:, s], src[:, s], mean(s), rstd(s), ALU.subtract, ALU.mult)
                    return last

                if p.stage in ("D1", "Y"):
                    slot = p.t % RING
                    m1 = mv1[:, slot]
                    r1 = rs1[:, slot]
                if p.stage == "D1":
                    wait("x_in", at("x_in"))
                    wait("s_ready", at("s_ready"))
                    stats(x_sb[:, slot], mv)
                    nc.vector.tensor_copy(m1, mv[:, :, :])
                    nc.vector.tensor_scalar(var2[:, 0], mv[:, :, 1], 1.0 + EPS, EPS * EPS, ALU.mult, ALU.add)
                    nc.vector.tensor_scalar(var2[:, 1], mv[:, :, 1], EPS, None, ALU.add).then_inc(S["var_ready"], 1)
                    wait("rstd_ready", at("rstd_ready", 1))
                    transposed()
                    normed(xhat, x_sb[:, slot], lambda s: m1[:, s, 0:1], lambda s: r1[:, 0, s:s + 1]).then_inc(S["xhat_ready"], 1)
                    if isinstance(p.t, int) and p.t == 0:
                        dve.wait_ge(w_in[7], 16)
                        nc.vector.tensor_copy(w_pj[:, 0], w_pj32).then_inc(split_done, 1)
                        dve.wait_ge(split_done, 1)
                        nc.vector.tensor_tensor(w_pj[:, 1], w_pj32, w_pj[:, 0].bitcast(f32), ALU.subtract).then_inc(split_done, 1)
                if p.stage == "D2":
                    wait("out_stored", at("out_stored"))
                    for j in range(2 * NC):
                        if j % NC == 0:
                            c = "qk"[j // NC]
                            wait(f"{c}_out", at(f"{c}_out"))
                        _, full, k = qk_bank(j)
                        free = full.replace("full", "free")
                        wait(free, at(free, k))
                        nc.vector.scalar_tensor_tensor(relub[:, j % 2], expb[:, j % 2], 1.0, relub[:, j % 2],
                                                       ALU.min, ALU.add).then_inc(S["feat_ready"], 1)
                        part = feat[:, j // NC, j % NC]
                        wait("feat_ready", at("feat_ready", 3 * j + 1))
                        nc.vector.tensor_copy(part[:, 0], relub[:, j % 2]).then_inc(S["feat_ready"], 1)
                        wait("feat_ready", at("feat_ready", 3 * j + 2))
                        nc.vector.tensor_tensor(part[:, 1], relub[:, j % 2], part[:, 0].bitcast(f32),
                                                ALU.subtract).then_inc(S["feat_ready"], 1)
                if p.stage == "B":
                    for r in range(ROUNDS):
                        for u in range(2):
                            for h in range(2):
                                if r >= 1 and h == 0:
                                    wait("am_used", at("am_used", 2 * (r - 1) + u + 1))
                                if r >= 1 and h == 1:
                                    wait(f"pq_full{u}", at(f"pq_full{u}", r))
                                wait(f"ps_full{u}", at(f"ps_full{u}", 2 * r + h + 1))
                                nc.vector.tensor_tensor(am[:, 2 * u + h].rearrange("p (g n) -> p g n", n=P),
                                                        ps[u][h][:, :].rearrange("p (g n) -> p g n", n=P),
                                                        mask[:, :].unsqueeze(1).broadcast_to([P, RG // 2, P]),
                                                        ALU.mult).then_inc(S[f"ps_free{u}"], 1)
                if p.stage in ("C1", "C2"):
                    for k, m in hidden_chunks(p):
                        wait(f"pq_free{m % 2}", at(f"pq_free{m % 2}", k // 2 + 1))
                        nc.vector.tensor_tensor(hidden[:, 1, m], gelub[:, m % 2], hidden[:, 0, m].bitcast(f32),
                                                ALU.subtract).then_inc(S["rest_ready"], 1)
                if p.stage == "A1":
                    wait("den_in", at("den_in"))
                    link(nc.vector.tensor_scalar(den[:, :], den[:, :], DEN_EPS, None, ALU.add))
                    nc.vector.reciprocal(den[:, :], den[:, :]).then_inc(S["rden_ready"], 1)
                if p.stage == "N":
                    wait("num_in", at("num_in"))
                    wait("rden_in", at("rden_in"))
                    nc.vector.tensor_tensor(attnT[:, :, :], num, rden.unsqueeze(1).broadcast_to([P, NC, T]),
                                            ALU.mult).then_inc(S["attnT_ready"], 1)
                if p.stage == "Y":
                    wait("s_ready", at("s_ready"))
                    transposed()
                    normed(x1, x_sb[:, slot], lambda s: m1[:, s, 0:1], lambda s: r1[:, 1, s:s + 1]).then_inc(S["y_ready"], 1)
                if p.stage == "A2":
                    wait("yb_ready", at("yb_ready"))
                    for u in range(2):
                        wait("ps_full1", at("ps_full1", u + 1))
                        o = x1[:, 2 * u:2 * u + 2].rearrange("p s d -> p (s d)")
                        nc.vector.tensor_tensor(o, o, ps[1][u][:, :], ALU.add).then_inc(S["ps_free1"], 1)
                    wait("ps_free1", at("ps_free1", 2))
                    stats(x1, mv)
                    nc.vector.tensor_scalar(var2[:, 0], mv[:, :, 1], EPS, None, ALU.add).then_inc(S["var_ready"], 1)
                if p.stage == "R":
                    wait("rstd_ready", at("rstd_ready"))
                    transposed()
                    normed(hn, x1, lambda s: mv[:, s, 0:1], lambda s: rs[:, s:s + 1]).then_inc(S["h_ready"], 1)
                if p.stage == "J":
                    wait("s_ready", at("s_ready"))
                    x2 = x2_sb[:, p.t % RING]
                    for u in range(2):
                        wait("ps_full0", at("ps_full0", u + 1))
                        nc.vector.tensor_tensor(x2[:, 2 * u:2 * u + 2], ps[0][u][:, :].rearrange("p (s d) -> p s d", d=D),
                                                x_sb[:, p.t % RING, 2 * u:2 * u + 2], ALU.add).then_inc(S["ps_free0"], 1)
                    wait("ps_free0", at("ps_free0", 2))
                    stats(x2, mv)
                    nc.vector.tensor_scalar(var2[:, 0], mv[:, :, 1], EPS, None, ALU.add).then_inc(S["var_ready"], 1)
                    wait("rstd_ready", at("rstd_ready", 1))
                    transposed()
                    normed(z, x2, lambda s: mv[:, s, 0:1], lambda s: rs[:, s:s + 1]).then_inc(S["z_ready"], 1)
                if p.stage == "G":
                    transposed()
                    link(nc.vector.reduce_sum(gs[:, 0:NC], pooled[:, :, :], AX))
                    for c in range(NC):
                        last = nc.vector.tensor_copy(pb128[:, c], gs[:, c:c + 1].broadcast_to([P, P]))
                    last.then_inc(S["pool_ready"], 1)
                    wait("pt_full0", at("pt_full0", 1))
                    link(nc.vector.scalar_tensor_tensor(g8[:, LOGIT], pt[0][:, 0:E], 1.0 / SEQ, row[:, 2 * D:2 * D + E],
                                                        ALU.mult, ALU.add))
                    hold()
                    link(nc.vector.max(g8[:, TOP8], g8[:, LOGIT]))
                    nc.vector.tensor_scalar(g8[:, SHIFTED], g8[:, LOGIT], g8[:, TOP8, 0:1], None,
                                            ALU.subtract).then_inc(S["logit_ready"], 1)
                    link(nc.vector.tensor_scalar(g8[:, CHOSEN], g8[:, LOGIT], g8[:, TOP8, 1:2], None, ALU.is_ge))
                    link(nc.vector.tensor_tensor(g8[:, RANK], g8[:, CHOSEN], row[:, 2 * D + E:2 * D + 2 * E], ALU.mult))
                    hold()
                    link(nc.vector.max(g8[:, RANK8], g8[:, RANK]))
                    nc.vector.tensor_scalar(choice[:, 0:TOP], g8[:, RANK8, 0:TOP], -1.0, float(E), ALU.mult, ALU.add)
                    link(nc.vector.tensor_scalar(choice[:, TOP:TOP + 1], g8[:, RANK8, TOP:TOP + 1], 0.0, None, ALU.is_gt))
                    link(nc.vector.tensor_scalar(choice[:, 0:TOP], choice[:, 0:TOP], float(E - 1), None, ALU.min))
                    wait("out_stored", at("out_stored"))
                    wait("chosen_in", at("chosen_in"))
                    nc.vector.tensor_copy(choice_i[:, 0:3], choice[:, 0:3]).then_inc(S["choice_ready"], 1)
                    wait("gexp_ready", at("gexp_ready", 1))
                    link(nc.vector.tensor_tensor(g8[:, EXP], g8[:, EXP], g8[:, CHOSEN], ALU.mult))
                    link(nc.vector.reduce_sum(gs[:, 2:3], g8[:, EXP], AX))
                    link(nc.vector.reciprocal(gs[:, 3:4], gs[:, 2:3]))
                    link(nc.vector.tensor_scalar(g8[:, GATE], g8[:, EXP], gs[:, 3:4], None, ALU.mult))
                    nc.vector.scalar_tensor_tensor(g8[:, REST], g8[:, RANK], g8[:, RANK8, TOP - 1:TOP], g8[:, GATE],
                                                   ALU.is_lt, ALU.mult)
                    for n in range(TOP):
                        last = nc.vector.scalar_tensor_tensor(g8[:, ONE + n], g8[:, RANK], g8[:, RANK8, n:n + 1],
                                                              g8[:, GATE], ALU.is_equal, ALU.mult)
                    link(last)
                    nc.vector.reduce_sum(gtop[:, :], g8[:, ONE:ONE + TOP], AX).then_inc(S["pt_free0"], 1)
                if p.stage == "F1":
                    wait("pt_free0", at("pt_free0"))
                    wait("k_out", at("k_out"))
                    for j in range(2 * TOP):
                        e, m = j // 2, j % 2
                        wait(f"pq_free{m}", at(f"pq_free{m}", e + 1))
                        if e == 0:
                            ins = nc.vector.tensor_scalar(acc[:, m], ge[:, m], gtop[:, 0:1], None, ALU.mult)
                        else:
                            wait("acc_ready", at("acc_ready", j - 1))
                            ins = nc.vector.scalar_tensor_tensor(acc[:, m], ge[:, m], gtop[:, e:e + 1], acc[:, m],
                                                                 ALU.mult, ALU.add)
                        ins.then_inc(S["acc_ready"], 1)
                    more = more_chosen(dve)
                    with dve.If(more > 0):
                        with dve.Fori(0, E) as e:
                            for m in range(NC):
                                dve.wait_ge(S["x_ge"], at("x_ge", 2 * e + m + 1))
                                nc.vector.scalar_tensor_tensor(acc[:, m], ge[:, m], g8[:, REST, bass.ds(e, 1)], acc[:, m],
                                                               ALU.mult, ALU.add).then_inc(S["x_sum"], 1)
                    with dve.Else():
                        dve.sem_inc(S["x_sum"], 2 * E)
                if p.stage == "F2":
                    wait("q_out", at("q_out"))
                    wait("out_stored", at("out_stored"))
                    for u in range(2):
                        wait(f"pt_full{u}", at(f"pt_full{u}", 1))
                        nc.vector.tensor_tensor(out_sb[:, 2 * u:2 * u + 2], pt[u][:, :].rearrange("p (s d) -> p s d", d=D),
                                                x2_sb[:, p.t % RING, 2 * u:2 * u + 2], ALU.add).then_inc(S[f"pt_free{u}"], 1)

            walk(dve, run)

        @block.tensor
        def _(pe):
            wait = waiter(pe)
            for n in (0, 1, 2, 5):
                pe.wait_ge(w_in[n], 16)
            for n in range(3 * NC + NM):
                for c in range(NC):
                    if n < 3 * NC:
                        w, b = w_qkv[:, n // NC, c, P * (n % NC):P * (n % NC + 1)], ln1b[:, c:c + 1]
                    else:
                        w, b = w_fc[:, c, P * (n - 3 * NC):P * (n - 3 * NC + 1)], ln2b[:, c:c + 1]
                    last = nc.tensor.matmul(pt[0][:, n:n + 1], w, b, start=(c == 0), stop=(c == NC - 1))
            last.then_inc(S["pt_full0"], 1)
            pe.wait_ge(fold_done, 1)
            for n in range(6, 9):
                pe.wait_ge(w_in[n], 16)

            def run(p):
                at = p.at

                def bank_q(n, k):
                    wait(f"pq_free{n}", at(f"pq_free{n}", k))

                def transposes(src):
                    for c in range(NC):
                        wait(f"pt_free{c}", at(f"pt_free{c}"))
                        for s in range(SUB):
                            last = nc.tensor.transpose(pt[c][:, P * s:P * (s + 1)], src[:, s, P * c:P * (c + 1)], ident[:, :])
                        last.then_inc(S[f"pt_full{c}"], 1)

                def copied(k):
                    for c in range(2):
                        wait(f"pt_free{c}", at(f"pt_free{c}", k))

                if p.stage == "X":
                    wait("xhat_ready", at("xhat_ready"))
                    transposes(xhat)
                if p.stage == "D2":
                    copied(0)
                    for j in (4, 5, 0, 1, 2, 3):
                        if j >= 2 * NC:
                            bank, full, k = pq[j % 2], f"pq_full{j % 2}", 1
                        else:
                            bank, full, k = qk_bank(j)
                        free = full.replace("full", "free")
                        wait(free, at(free, 0 if full == "ps_full1" else k - 1))
                        for c in range(NC):
                            last = nc.tensor.matmul(bank[:, :], w_qkv[:, j // NC, c, P * (j % NC):P * (j % NC + 1)],
                                                    xhT[:, c], start=(c == 0), stop=(c == NC - 1))
                        last.then_inc(S[full], 1)
                if p.stage == "VT":
                    wait("v_in", at("v_in"))
                    for u in range(4):
                        wait(f"pt_free{u % 2}", at(f"pt_free{u % 2}", u // 2))
                        for g in range(4):
                            last = nc.tensor.transpose(pt[u % 2][:, P * g:P * (g + 1)],
                                                       vd[:, :, :, :].rearrange("p b h t -> p (b h t)")[:, 4 * u + g::GG // 2], ident[:, :])
                        last.then_inc(S[f"pt_full{u % 2}"], 1)
                if p.stage == "B":
                    copied(0)
                    wait("q_in", at("q_in"))
                    wait("k_in", at("k_in"))

                    def score(r, u, h, g):
                        rows, gg = slice(64 * h, 64 * h + KP), RG * r + g
                        lo = P * (g % (RG // 2))
                        return nc.tensor.matmul(ps[u][h][:, lo:lo + P], kd[rows, gg::GG], qd[rows, gg::GG],
                                                start=True, stop=True)

                    def weighted(r, h, g):
                        lo = P * (g % (RG // 2))
                        return nc.tensor.matmul(pq[g // (RG // 2)][32 * h:32 * h + 32, lo:lo + P], vb[:, GG * h + RG * r + g],
                                                am[:, 2 * (g // (RG // 2)) + h, lo:lo + P], start=True, stop=True)

                    for r in range(ROUNDS + 1):
                        for u in range(2):
                            if r >= 1:
                                bank_q(u, r - 1)
                            for h in range(2):
                                wait(f"ps_free{u}", at(f"ps_free{u}", max(2 * r + h - 1, 0)))
                                for g in range(RG // 2 * u, RG // 2 * (u + 1)):
                                    if r < ROUNDS:
                                        last = score(r, u, h, g)
                                        if g % (RG // 2) == RG // 2 - 1:
                                            last.then_inc(S[f"ps_full{u}"], 1)
                                    if r >= 1:
                                        last = weighted(r - 1, h, g)
                                if r >= 1:
                                    last.then_inc(S["am_used" if h == 0 else f"pq_full{u}"], 1)
                if p.stage == "A2":
                    wait("attnT_ready", at("attnT_ready"))
                    wait("ps_free1", at("ps_free1"))
                    for u in range(2):
                        for s in range(2):
                            for c in range(NC):
                                lo = P * (2 * u + s)
                                last = nc.tensor.matmul(ps[1][u][:, D * s:D * (s + 1)], attnT[:, c, lo:lo + P], w_o[:, c],
                                                        start=(c == 0), stop=(c == NC - 1))
                        last.then_inc(S["ps_full1"], 1)
                if p.stage == "H":
                    wait("h_ready", at("h_ready"))
                    transposes(hn)
                if p.stage in ("C1", "C2"):
                    for k, m in hidden_chunks(p):
                        bank_q(m % 2, k // 2)
                        for c in range(NC):
                            if m == 0:
                                wait(f"pt_free{c}", at(f"pt_free{c}"))
                            last = nc.tensor.matmul(pq[m % 2][:, :], w_fc[:, c, P * m:P * (m + 1)], hT[:, c],
                                                    start=(c == 0), stop=(c == NC - 1))
                        last.then_inc(S[f"pq_full{m % 2}"], 1)
                if p.stage == "J":
                    wait("rest_ready", at("rest_ready"))
                    wait("ps_free0", at("ps_free0"))
                    if isinstance(p.t, int) and p.t == 0:
                        pe.wait_ge(split_done, 2)
                    for u in range(2):
                        for s in range(2):
                            lo = P * (2 * u + s)
                            for n, ((a, b), m) in enumerate((ab, m) for ab in sorted(TERMS) for m in range(NM)):
                                last = nc.tensor.matmul(ps[0][u][:, D * s:D * (s + 1)], hidden[:, a, m, lo:lo + P],
                                                        w_pj[:, b, m], start=(n == 0), stop=(n == len(TERMS) * NM - 1))
                        last.then_inc(S["ps_full0"], 1)
                if p.stage == "E":
                    wait("z_ready", at("z_ready"))
                    transposes(z)
                if p.stage == "G":
                    wait("pool_ready", at("pool_ready", 1))
                    wait("pt_free0", at("pt_free0"))
                    for c in range(NC):
                        last = nc.tensor.matmul(pt[0][:, 0:E], pb128[:, c], w_g[:, c], start=(c == 0), stop=(c == NC - 1))
                    last.then_inc(S["pt_full0"], 1)
                if p.stage == "F1":
                    copied(-1)
                    wait("chosen_in", at("chosen_in"))

                    def expert(w, m):
                        for c in range(NC):
                            last = nc.tensor.matmul(pq[m][:, :], w[:, c, P * m:P * (m + 1)], zT[:, p.t % RING, c],
                                                    start=(c == 0), stop=(c == NC - 1))
                        return last

                    for e in range(TOP):
                        for m in range(NC):
                            bank_q(m, e)
                            expert(w_e[:, e], m).then_inc(S[f"pq_full{m}"], 1)
                    more = more_chosen(pe)
                    with pe.If(more > 0):
                        bank_q(0, TOP)
                        bank_q(1, TOP)
                        pe.sem_inc(held, 1)
                        with pe.Fori(0, E) as e:
                            pe.wait_ge(S["xw_in"], at("xw_in", 32 * e + 32))
                            pe.wait_ge(S["x_sum"], at("x_sum", 2 * e))
                            for m in range(NC):
                                expert(w_x, m).then_inc(S["x_mm"], 1)
                        wait("x_sum", at("x_sum", 2 * E))
                    with pe.Else():
                        pe.sem_inc(S["x_mm"], 2 * E)
                if p.stage == "F2":
                    wait("acc_ready", at("acc_ready"))
                    for u in range(2):
                        wait(f"pt_free{u}", at(f"pt_free{u}"))
                        for s in range(2):
                            for m in range(NC):
                                lo = P * (2 * u + s)
                                last = nc.tensor.transpose(pt[u][:, D * s + P * m:D * s + P * (m + 1)],
                                                           acc[:, m, lo:lo + P], ident[:, :])
                        last.then_inc(S[f"pt_full{u}"], 1)

            walk(pe, run)


def kernel(**inputs):
    import concourse.bacc as bacc
    from concourse.bass_utils import run_bass_kernel_spmd

    get = {k.replace("L0_", ""): np.asarray(v) for k, v in inputs.items()}

    def chunks(w):
        return np.moveaxis(w.reshape(-1, P, *w.shape[1:]), 1, 0)

    arrays = {
        "x": get["attn_q_x"].reshape(BATCH * SEQ, D),
        "wqkv": np.stack([chunks(get["attn_w" + n]) for n in "qkv"], 1),
        "wo": chunks(get["attn_wo"].reshape(H, HD, D).transpose(1, 0, 2).reshape(D, D)),
        "fcw": chunks(get["attn_fc_w"]),
        "pjw": chunks(get["attn_proj_w"]),
        "gw": chunks(get["ffn_gate_w"].T),
        "ew": np.stack([chunks(w.T) for w in get["ffn_expert_w"]], 1),
        "eb": np.stack([chunks(b) for b in get["ffn_expert_b"]], 1),
        "cols": np.concatenate([chunks(get[n]) for n in (
            "attn_ln1_w", "attn_ln1_b", "attn_ln2_w", "attn_ln2_b", "attn_bq", "attn_bk", "attn_bv", "attn_fc_b")], 1),
        "rows": np.tile(np.concatenate([get["attn_bo"], get["attn_proj_b"], get["ffn_gate_b"],
                                         np.arange(E, 0, -1, dtype=np.float32)])[None], (P, 1)),
        "ident": np.eye(P, dtype=np.float32),
        "mask": ((np.arange(P)[:, None] % TB == np.arange(P)[None] % TB)
                 & (np.arange(P)[:, None] // 64 == np.arange(P)[None] // 64)).astype(np.float32),
    }
    nc = bacc.Bacc("TRN2", target_bir_lowering=False, num_devices=1)
    maps, args = {}, []
    for name, a in arrays.items():
        a = np.ascontiguousarray(a)
        maps[f"in_{name}"] = a
        args.append(nc.dram_tensor(f"in_{name}", a.shape, mybir.dt.from_np(a.dtype), kind="ExternalInput").ap())
    out = nc.dram_tensor("out", (BATCH * SEQ, D), mybir.dt.float32, kind="ExternalOutput").ap()
    build(nc, *args, out)
    r = run_bass_kernel_spmd(nc, [maps], core_ids=[0])
    return r.results[0]["out"].reshape(BATCH, SEQ, D)
```

```python
import numpy as np
from contextlib import ExitStack

import concourse.bass as bass
from concourse import mybir

BATCH, SEQ, D = 4, 2048, 256
H, HD = 16, 16
MLP = 4 * D
E = 8
TOP = 2
P = 128
NC = D // P
NM = MLP // P
T = 512
SUB = T // P
TILES = BATCH * SEQ // T
PER_BATCH = SEQ // T
RING = 4
NQ = 4
QT = T // NQ
TB = 4
GG = QT // TB
RG = 8
ROUNDS = GG // RG
K_PARTS, Q_PARTS = (0, 1, 0), (0, 0, 1)
KP = HD * len(K_PARTS)
TERMS = tuple(zip(K_PARTS, Q_PARTS))
UP = {"C1": (0, 4), "C2": (4, 6), "C3": (6, 8)}
EPS = 1e-5
DEN_EPS = 1e-6

LAG = {"L": 0, "DS": 0, "D1": 0, "X": 0, "D2": 0, "QK": 0, "VT": 0, "B0": 1, "B": 1, "A1": 1, "N": 1, "Y": 1, "A2": 1,
       "R": 2, "H": 2, "C1": 2, "C2": 2, "C3": 2, "J": 2, "E": 2, "F1": 6, "FX": 6, "F2": 6}
FULL = ["L", "F1", "B0", "FX", "B", "R", "F2", "H", "DS", "C1", "D1", "C2", "X", "C3",
        "A1", "D2", "N", "Y", "J", "QK", "A2", "VT", "E"]
HEAD = ["L", "W", "B0", "B", "R", "H", "DS", "C1", "D1", "C2", "X", "G", "C3",
        "A1", "F1", "FX", "F2", "D2", "N", "Y", "J", "QK", "A2", "VT", "E"]

INC = {
    "pt_full0": {"P": 1, "X": 1, "VT": 2, "H": 1, "E": 1, "F2": 1, "G": 1},
    "pt_free0": {"P": 1, "X": 1, "VT": 2, "H": 1, "E": 1, "F2": 1, "G": 1},
    "pt_full1": {"X": 1, "VT": 2, "H": 1, "E": 1, "F2": 1},
    "pt_free1": {"X": 1, "VT": 2, "H": 1, "E": 1, "F2": 1},
    "pq_full0": {"D2": 2, "J": 1, "B": 4, "C1": 2, "C2": 1, "C3": 1, "F1": TOP},
    "pq_free0": {"D2": 2, "J": 1, "B": 4, "C1": 2, "C2": 1, "C3": 1, "F1": TOP},
    "pq_full1": {"D2": 2, "J": 1, "B": 4, "C1": 2, "C2": 1, "C3": 1, "F1": TOP},
    "pq_free1": {"D2": 2, "J": 1, "B": 4, "C1": 2, "C2": 1, "C3": 1, "F1": TOP},
    "am_used": {"B": 8},
    "ps_full0": {"B0": 2, "B": 6, "J": 2}, "ps_free0": {"B0": 2, "B": 6, "J": 2},
    "ps_full1": {"B0": 2, "B": 6, "A2": 2, "D2": 2}, "ps_free1": {"B0": 2, "B": 6, "A2": 2, "D2": 2},
    "x_in": {"L": 16},
    "var_ready": {"DS": 1, "A2": 1, "J": 1},
    "rstd_ready": {"DS": 1, "A2": 1, "J": 1},
    "xhat_ready": {"D1": 1},
    "feat_ready": {"D2": 12},
    "q_out": {"D2": 32}, "k_out": {"D2": 32}, "v_out": {"D2": 16},
    "q_in": {"QK": 96}, "k_in": {"QK": 96}, "v_in": {"D2": 128},
    "nd_out": {"B": 64}, "num_in": {"B": 16}, "den_in": {"B": 16},
    "rden_ready": {"A1": 1}, "rden_out": {"A1": 16}, "rden_in": {"A1": 16 * P // H},
    "attnT_ready": {"N": 1},
    "y_ready": {"Y": 1}, "yb_ready": {"Y": 1}, "s_ready": {"P": 1, "A2": 1},
    "h_ready": {"R": 1}, "rest_used": {"J": 1}, "rest_ready": {"C1": 4, "C2": 2, "C3": 2}, "h_round": {"H": NC},
    "z_ready": {"J": 1},
    "pool_ready": {"G": 1}, "logit_ready": {"G": 1}, "gexp_ready": {"G": 1},
    "acc_ready": {"P": 1, "F1": 2, "FX": 2},
    "out_stored": {"P": 16, "F2": 16},
    "dve_chain": {"N": 2, "DS": 2, "A1": 1, "A2": 2, "J": 2, "G": 13},
    "xw_in": {"P": 16, "FX": 32 * E}, "x_mm": {"P": 1, "FX": 2 * E}, "x_ge": {"P": 1, "FX": 2 * E},
    "x_sum": {"P": 1, "FX": 2 * E},
    "choice_ready": {"G": 1}, "chosen_in": {"P": 16, "G": 64},
    "pool_chain": {"Y": 1},
}


class Place:

    def __init__(self, stage, i, base, rates):
        self.stage, self.i, self.base, self.rates = stage, i, base, rates
        self.t = i - LAG[stage] if stage in LAG else None

    def at(self, name, more=0):
        value = self.base.get(name, 0) + more
        for index, rate in self.rates:
            if rate.get(name, 0):
                value = index * rate[name] + value
        return value


def total(stages):
    out = {}
    for name, by in INC.items():
        out[name] = sum(by.get(s, 0) for s in stages)
    return out


def plus(a, b, times=1):
    return {k: a.get(k, 0) + times * b.get(k, 0) for k in INC}


def walk(eng, run):
    base = total(["P"])

    def stages(names, i, rates):
        nonlocal base
        for s in names:
            run(Place(s, i, base, rates))
            base = plus(base, total([s]))

    def loop(lo, hi, names):
        nonlocal base
        rate = total(names)
        at = base
        with eng.Fori(0, hi - lo) as k:
            stages(names, k + lo, [(k, rate)])
        base = plus(at, rate, hi - lo)

    def drop(*out):
        return ["L", "W"] + [s for s in FULL if s not in out + ("L",)]

    stages(["L", "DS", "D1", "X", "D2", "QK", "VT"], 0, [])
    stages(drop("F1", "FX", "F2", "R", "H", "C1", "C2", "C3", "J", "E"), 1, [])
    stages(drop("F1", "FX", "F2"), 2, [])
    loop(3, 6, drop("F1", "FX", "F2"))
    at, rate, head = base, total(FULL), total(HEAD)
    epoch = plus(head, rate, PER_BATCH - 1)
    with eng.Fori(0, 2) as e:
        stages(HEAD, e * PER_BATCH + 6, [(e, epoch)])
        with eng.Fori(0, PER_BATCH - 1) as k:
            stages(FULL, e * PER_BATCH + k + 7, [(e, epoch), (k, rate)])
    base = plus(at, epoch, 2)
    stages(HEAD, 14, [])
    stages(FULL, 15, [])
    stages([s for s in FULL if s not in ("L", "DS", "D1", "X", "D2", "QK", "VT")], 16, [])
    stages(["F1", "FX", "R", "F2", "H", "C1", "C2", "C3", "J", "E"], 17, [])
    stages(["G"], 0, [])
    loop(18, 22, ["F1", "FX", "F2"])


def build(nc, x, wqkv, wo, fcw, pjw, gw, ew, eb, cols, rows, ident_d, mask_d, out):
    f32 = mybir.dt.float32
    f32r = mybir.dt.float32r
    ALU = mybir.AluOpType
    ACT = mybir.ActivationFunctionType
    AX = mybir.AxisListType.X

    ctx = ExitStack()
    with ctx:
        def sb(name, shape, dt=f32):
            return ctx.enter_context(nc.sbuf_tensor(name, shape, dt))

        def sem(name):
            return ctx.enter_context(nc.semaphore(name))

        w_qkv = sb("w_qkv", [P, 3, NC, D])
        w_o = sb("w_o", [P, 2, NC, D], f32r)
        w_fc = sb("w_fc", [P, 2, NC, MLP], f32r)
        w_pj = sb("w_pj", [P, 2, NM, D], f32r)
        w_g = sb("w_g", [P, NC, E])
        w_e = sb("w_e", [P, TOP, NC, D])
        b_e = sb("b_e", [P, TOP + 1, NC])
        NCOL = 4 * NC + 3 * NC + NM
        col = sb("col", [P, NCOL])
        ln1w, ln1b, ln2w, ln2b = (col[:, NC * n:NC * (n + 1)] for n in range(4))
        b_qkv = col[:, 8:8 + 3 * NC]
        b_fc = col[:, 8 + 3 * NC:8 + 3 * NC + NM]
        row = sb("row", [P, 2 * D + 2 * E])
        ident = sb("ident", [P, P])
        mask = sb("mask", [P, P])
        mhalf = sb("mhalf", [P, 2 * SUB])
        x_sb = sb("x_sb", [P, RING, SUB, D])
        x2_sb = sb("x2_sb", [P, RING, SUB, D])
        w_pj32 = x2_sb[:, :, :, :].rearrange("p r s d -> p (r s) d")[:, 0:NM]
        w_fc32 = x2_sb[:, :, :, :].rearrange("p r s d -> p (r s d)")[:, NM * D:].rearrange("p (c m) -> p c m", c=NC)
        zT = sb("zT", [P, RING, NC, T])
        pooled = sb("pooled", [P, NC, RING])
        mv1 = sb("mv1", [P, RING, SUB, 2])
        rs1 = sb("rs1", [P, RING, 2, SUB])
        stat = sb("stat", [P, SUB, 6])
        mv = sb("mv", [P, SUB, 2])
        var2 = sb("var2", [P, 2, SUB])
        rs = sb("rs", [P, SUB])
        xhat = sb("xhat", [P, SUB, D])
        hn = sb("hn", [P, SUB, D])
        z = hn
        w_o32 = hn[:, 0:NC]
        xhT = sb("xhT", [P, NC, T])
        hT = sb("hT", [P, 2, NC, T], f32r)
        attnT = hT
        feat = sb("feat", [P, 2, NC, 2, T], f32r)
        feat_v = sb("feat_v", [P, NC, T])
        out_sb = feat[:, 0, 0].bitcast(f32).rearrange("p c t -> p (c t)").rearrange("p (s d) -> p s d", d=D)
        acc = feat[:, 1, 0].bitcast(f32)
        ge = feat_v
        hid = sb("hid", [P, 2, NM * T], f32r)
        hidden = hid[:, :, :].rearrange("p w (m t) -> p w m t", t=T)
        kd, qd = hid[:, 0], hid[:, 1]
        vb = sb("vb", [P, 2 * GG, 2 * HD])
        am = sb("am", [P, 4, 512])
        expb, relub = am[:, 0:2], am[:, 2:4]
        gelub = am[:, 0:2]
        ot = sb("ot", [P, H, T // 2])
        nd = ot[:, :, :].rearrange("p h t -> p (h t)").rearrange("p (n t) -> p n t", t=T)
        vd = ot[:, H // 2:].rearrange("p h t -> p (h t)").rearrange("p (h b t) -> p h b t", h=H, b=2)
        w_x = nd[:, NC + 1].rearrange("p (c d) -> p c d", c=NC)
        num, rden = nd[:, 0:NC], nd[:, NC]
        den = sb("den", [P, H * T // P])
        x1 = xhat
        pb128 = sb("pb128", [P, NC, P])
        held_at = sb("held_at", [P, 1])
        held_act = sb("held_act", [P, 2])
        g8 = sb("g8", [P, 11, E])
        LOGIT, TOP8, SHIFTED, EXP, CHOSEN, GATE, RANK, RANK8, REST, ONE = range(10)
        gs = sb("gs", [P, 4])
        gtop = sb("gtop", [P, TOP])
        choice = sb("choice", [P, 4])
        choice_i = ctx.enter_context(nc.sbuf_tensor("choice_i", [P, 4], mybir.dt.int32))

        pt = [ctx.enter_context(nc.psum_tensor(f"pt{n}", [P, 512], f32)) for n in range(2)]
        pq = [ctx.enter_context(nc.psum_tensor(f"pq{n}", [P, 512], f32)) for n in range(2)]
        ps = [[ctx.enter_context(nc.psum_tensor(f"ps{n}{p}", [P, 512], f32)) for p in range(2)] for n in range(2)]

        qk_dram = [nc.dram_tensor(f"scratch_{n}", (2, 2, D, T // 2), f32, kind="Internal").ap() for n in "qk"]
        v_dram = nc.dram_tensor("scratch_v", (D, T), f32, kind="Internal").ap()
        num_dram = nc.dram_tensor("scratch_num", (D, T), f32, kind="Internal").ap()
        den_dram = nc.dram_tensor("scratch_den", (H, T), f32, kind="Internal").ap()
        rden_dram = nc.dram_tensor("scratch_rden", (H, T), f32, kind="Internal").ap()

        S = {name: sem(name) for name in INC}
        w_in = [sem(f"w_in{n}") for n in range(9)]
        fold_done = sem("fold_done")
        const_done = sem("const_done")
        split_done = sem("split_done")

        x_t = x.rearrange("(n s p) d -> n p s d", s=SUB, p=P)
        out_t = out.rearrange("(n s p) d -> n p s d", s=SUB, p=P)

        block = ctx.enter_context(nc.Block())

        held = sem("held")

        def waiter(eng, own=False):
            def wait(name, value):
                if not isinstance(value, int) or value > 0:
                    eng.wait_ge(S[name], value)
                    if own and not isinstance(value, int):
                        eng.sem_inc(held, 1)
            return wait

        def qk_bank(j):
            if j < NC:
                return ps[1][j], "ps_full1", j + 1
            return pq[j - NC], f"pq_full{j - NC}", 2

        def hidden_chunks(p):
            return enumerate(range(*UP[p.stage]))

        def down_bank(u, s):
            return ps[0][u] if s == 0 else pq[u]

        def more_chosen(eng):
            return eng.value_load(choice_i[0:1, TOP:TOP + 1], min_val=0, max_val=1)

        @block.sync
        def _(sp):
            wait = waiter(sp, own=True)
            for n, (dst, src) in enumerate([
                (ident[:, :], ident_d), (col[:, :], cols), (w_qkv[:, :, :, :], wqkv), (row[:, :], rows),
                (mask[:, :], mask_d), (w_fc32, fcw), (w_o32, wo), (w_pj32, pjw),
                (w_g[:, :, :], gw),
            ]):
                sp.dma_start(dst, src).then_inc(w_in[n], 16)

            def run(p):
                at = p.at
                if p.stage == "L":
                    wait("xhat_ready", at("xhat_ready"))
                    sp.dma_start(x_sb[:, p.t % RING], x_t[p.t]).then_inc(S["x_in"], 16)
                if p.stage == "D2":
                    wait("v_in", at("v_in"))
                    for b in range(2):
                        wait(f"pq_free{b}", at(f"pq_free{b}", 1))
                    sp.dma_start(v_dram.rearrange("(c p) t -> p c t", p=P), feat_v[:, :, :]).then_inc(S["v_out"], 16)
                    for n, c in enumerate("qk"):
                        wait(f"{c}_in", at(f"{c}_in"))
                        for m in range(NC):
                            wait("feat_ready", at("feat_ready", 3 * (NC * n + m + 1)))
                            sp.dma_start(qk_dram[n].rearrange("w f (c p) t -> c p (w f) t", p=P)[m],
                                         feat[:, n, m].bitcast(f32).rearrange("p w (f t) -> p (w f) t", f=2)
                                         ).then_inc(S[f"{c}_out"], 16)
                        if n == 0:
                            wait("v_out", at("v_out", 16))
                            if isinstance(p.t, int) and p.t == 0:
                                sp.wait_ge(const_done, 4)
                            for j in range(NQ):
                                src = v_dram.rearrange("(h d) (p b j t) -> p j b d h t", d=HD, p=2, b=2, j=2)
                                for b in range(2):
                                    sp.dma_start(vd[32 * j:32 * j + HD, :, b], src[j // 2, j % 2, b]).then_inc(S["v_in"], 16)
                if p.stage == "QK":
                    wait("ps_full1", at("ps_full1"))
                    for n, c, dst, parts, used in ((0, "q", qd, Q_PARTS, ["rest_used"]),
                                                  (1, "k", kd, K_PARTS, ["pq_full0", "pq_full1"])):
                        for name in used:
                            wait(name, at(name))
                        wait(f"{c}_out", at(f"{c}_out"))
                        for hf in range(2):
                            for r, w in enumerate(parts):
                                lo = 64 * hf + HD * r
                                sp.dma_start(dst[lo:lo + HD].bitcast(f32), qk_dram[n][w, hf].rearrange("(d h) t -> d (h t)", h=H)
                                             ).then_inc(S[f"{c}_in"], 16)
                if p.stage == "B":
                    for b in range(2):
                        wait(f"pq_free{b}", at(f"pq_free{b}", ROUNDS))
                    for f in range(2):
                        ts = slice(T // 2 * f, T // 2 * (f + 1))
                        sp.dma_start(den_dram.rearrange("(o h) t -> o h t", o=1)[:, :, ts],
                                     ot[32 * f + HD:32 * f + HD + 1]).then_inc(S["nd_out"], 16)
                        sp.dma_start(num_dram.rearrange("(e h) t -> e h t", h=H)[:, :, ts],
                                     ot[32 * f:32 * f + HD]).then_inc(S["nd_out"], 16)
                    wait("nd_out", at("nd_out", 64))
                    sp.dma_start(den[:, :], den_dram.rearrange("h (a b) -> (h a) b", b=H * T // P)).then_inc(S["den_in"], 16)
                    sp.dma_start(num, num_dram.rearrange("(c p) t -> p c t", p=P)).then_inc(S["num_in"], 16)
                if p.stage == "A1":
                    wait("rden_ready", at("rden_ready", 1))
                    sp.dma_start(rden_dram.rearrange("h (a b) -> (h a) b", b=H * T // P), den[:, :]).then_inc(S["rden_out"], 16)
                    wait("rden_out", at("rden_out", 16))
                    for e in range(P // H):
                        sp.dma_start(rden[H * e:H * (e + 1)], rden_dram).then_inc(S["rden_in"], 16)
                if p.stage == "FX":
                    wait("choice_ready", at("choice_ready"))
                    more = more_chosen(sp)
                    with sp.If(more > 0):
                        with sp.Fori(0, E) as e:
                            sp.wait_ge(S["x_sum"], at("x_sum", 2 * e))
                            sp.sem_inc(held, 1)
                            sp.dma_start(w_x, ew[:, e]).then_inc(S["xw_in"], 16)
                            sp.dma_start(b_e[:, TOP], eb[:, e]).then_inc(S["xw_in"], 16)
                    with sp.Else():
                        sp.sem_inc(S["xw_in"], 32 * E)
                if p.stage == "F2":
                    for u in range(2):
                        wait(f"pt_free{u}", at(f"pt_free{u}", 1))
                    sp.dma_start(out_t[p.t], out_sb).then_inc(S["out_stored"], 16)

            walk(sp, run)
            sp.wait_ge(S["out_stored"], 16 * (TILES + 1))

        @block.gpsimd
        def _(pool):
            wait = waiter(pool)
            nc.gpsimd.memset(mhalf[:, :], -0.5).then_inc(const_done, 1)
            nc.gpsimd.memset(vd[:, :, :, :], 0.0).then_inc(const_done, 1)
            nc.gpsimd.memset(vb[:, :, :], 1.0).then_inc(const_done, 1)
            nc.gpsimd.memset(held_act[:, :], 0.0).then_inc(const_done, 1)
            pool.wait_ge(w_in[3], 16)

            pool.sem_inc(S["s_ready"], 1)
            pool.sem_inc(S["acc_ready"], 1)
            pool.sem_inc(S["out_stored"], 16)
            for name in ("x_mm", "x_ge", "x_sum"):
                pool.sem_inc(S[name], 1)
            pool.sem_inc(S["xw_in"], 16)
            pool.sem_inc(S["chosen_in"], 16)

            def rows_of(lo):
                return row[:, lo:lo + D].unsqueeze(1).broadcast_to([P, SUB, D])

            def run(p):
                at = p.at
                if p.stage == "DS":
                    wait("var_ready", at("var_ready", 1))
                    nc.gpsimd.tensor_tensor(rs1[:, p.t % RING], var2[:, :, :],
                                            mhalf[:, :].rearrange("p (a s) -> p a s", a=2), ALU.pow).then_inc(S["rstd_ready"], 1)
                if p.stage == "Y":
                    wait("y_ready", at("y_ready", 1))
                    nc.gpsimd.tensor_tensor(x1[:, :, :], x1[:, :, :], rows_of(0), ALU.add).then_inc(S["yb_ready"], 1)
                    slot = x_sb[:, p.t % RING]
                    nc.gpsimd.tensor_tensor(slot, slot, rows_of(D), ALU.add).then_inc(S["pool_chain"], 1)
                if p.stage == "A2":
                    slot = x_sb[:, p.t % RING]
                    wait("var_ready", at("var_ready", 1))
                    nc.gpsimd.tensor_tensor(rs[:, :], var2[:, 0], mhalf[:, 0:SUB], ALU.pow).then_inc(S["rstd_ready"], 1)
                    wait("ps_free1", at("ps_free1", 2))
                    wait("pool_chain", at("pool_chain"))
                    pool.sem_inc(held, 1)
                    nc.gpsimd.tensor_tensor(slot, slot, x1[:, :, :], ALU.add).then_inc(S["s_ready"], 1)
                if p.stage == "J":
                    wait("var_ready", at("var_ready", 1))
                    nc.gpsimd.tensor_tensor(rs[:, :], var2[:, 0], mhalf[:, 0:SUB], ALU.pow).then_inc(S["rstd_ready"], 1)

            walk(pool, run)

        @block.scalar
        def _(act):
            wait = waiter(act)
            act.wait_ge(fold_done, 1)
            act.wait_ge(const_done, 4)

            def run(p):
                at = p.at
                if p.stage == "X":
                    for c in range(NC):
                        wait(f"pt_full{c}", at(f"pt_full{c}", 1))
                        nc.scalar.activation(xhT[:, c], pt[c][:, :], ACT.Identity).then_inc(S[f"pt_free{c}"], 1)
                if p.stage == "D2":
                    nc.scalar.activation(held_act[:, 1:2], held_act[:, 0:1], ACT.Exp)
                    wait("acc_ready", at("acc_ready"))
                    wait("v_out", at("v_out"))
                    for m in range(NC):
                        wait(f"pq_full{m}", at(f"pq_full{m}", 1))
                        dst = feat_v[:, m].rearrange("p (q j t g) -> p j q t g", q=NQ, j=2, t=TB)
                        src = pq[m][:, :].rearrange("p (q t j g) -> p j q t g", q=NQ, j=2, t=TB)
                        for half in range(2):
                            last = nc.scalar.activation(dst[:, half], src[:, half], ACT.Identity,
                                                        bias=b_qkv[:, 2 * NC + m:2 * NC + m + 1])
                        last.then_inc(S[f"pq_free{m}"], 1)
                    wait("rest_ready", at("rest_ready"))
                    for j in range(2 * NC):
                        bank, full, k = qk_bank(j)
                        wait(full, at(full, k))
                        wait("feat_ready", at("feat_ready", 3 * max(j - 1, 0)))
                        nc.scalar.activation(expb[:, j % 2], bank[:, :], ACT.Exp, bias=b_qkv[:, j:j + 1])
                        nc.scalar.activation(relub[:, j % 2], bank[:, :], ACT.Relu,
                                             bias=b_qkv[:, j:j + 1]).then_inc(S[full.replace("full", "free")], 1)
                if p.stage == "VT":
                    for u in range(4):
                        wait(f"pt_full{u % 2}", at(f"pt_full{u % 2}", u // 2 + 1))
                        src = pt[u % 2][:, :].rearrange("p (g j e) -> p j g e", g=4, j=NQ)[:, :, :, 0:HD]
                        dst = vb[:, :, :].rearrange("p (j g) e -> p j g e", j=NQ)[:, :, 4 * u:4 * u + 4, 0:HD]
                        nc.scalar.activation(dst, src, ACT.Identity).then_inc(S[f"pt_free{u % 2}"], 1)
                if p.stage == "B":
                    wait("attnT_ready", at("attnT_ready"))
                    rows = slice(0, 64)
                    for r in range(ROUNDS):
                        for u in range(2):
                            wait(f"pq_full{u}", at(f"pq_full{u}", r + 1))
                            dst = ot[rows].rearrange("p h (a g) -> p g (h a)", g=GG)
                            src = pq[u][rows, :].rearrange("p (g a) -> p g a", g=RG // 2)
                            lo = RG * r + RG // 2 * u
                            nc.scalar.activation(dst[:, lo:lo + RG // 2], src, ACT.Identity).then_inc(S[f"pq_free{u}"], 1)
                if p.stage == "H":
                    for c in range(NC):
                        wait(f"pt_full{c}", at(f"pt_full{c}", 1))
                        nc.scalar.activation(hT[:, 0, c], pt[c][:, :], ACT.Identity).then_inc(S["h_round"], 1)
                if p.stage in UP:
                    for k, m in hidden_chunks(p):
                        wait(f"pq_full{m % 2}", at(f"pq_full{m % 2}", k // 2 + 1))
                        wait("rest_ready", at("rest_ready", max(k - 1, 0) if p.stage == "C1" else k - 1))
                        nc.scalar.activation(gelub[:, m % 2], pq[m % 2][:, :], ACT.Gelu, bias=b_fc[:, m:m + 1])
                        nc.scalar.activation(hidden[:, 0, m], pq[m % 2][:, :], ACT.Gelu,
                                             bias=b_fc[:, m:m + 1]).then_inc(S[f"pq_free{m % 2}"], 1)
                if p.stage == "E":
                    for c in range(NC):
                        wait(f"pt_full{c}", at(f"pt_full{c}", 1))
                        nc.scalar.activation(zT[:, p.t % RING, c], pt[c][:, :], ACT.Identity,
                                             accum_out=pooled[:, c, bass.ds(p.t % RING, 1)]).then_inc(S[f"pt_free{c}"], 1)
                if p.stage == "G":
                    wait("logit_ready", at("logit_ready", 1))
                    nc.scalar.activation(g8[:, EXP], g8[:, SHIFTED], ACT.Exp).then_inc(S["gexp_ready"], 1)
                    wait("acc_ready", at("acc_ready"))
                    wait("x_sum", at("x_sum"))
                    wait("choice_ready", at("choice_ready", 1))
                    act.sem_inc(held, 1)
                    for n in range(TOP):
                        e = act.value_load(choice_i[0:1, n:n + 1], min_val=0, max_val=E - 1)
                        act.dma_start(w_e[:, n], ew[:, e]).then_inc(S["chosen_in"], 16)
                        act.dma_start(b_e[:, n], eb[:, e]).then_inc(S["chosen_in"], 16)
                if p.stage == "F1":
                    nc.scalar.activation(held_act[:, 1:2], held_act[:, 0:1], ACT.Gelu)
                    wait("v_out", at("v_out"))
                    wait("chosen_in", at("chosen_in"))
                    for e in range(TOP):
                        for m in range(NC):
                            wait(f"pq_full{m}", at(f"pq_full{m}", e + 1))
                            wait("acc_ready", at("acc_ready", max(2 * e + m - 1, 0)))
                            nc.scalar.activation(ge[:, m], pq[m][:, :], ACT.Gelu,
                                                 bias=b_e[:, e, m:m + 1]).then_inc(S[f"pq_free{m}"], 1)
                if p.stage == "FX":
                    more = more_chosen(act)
                    with act.If(more > 0):
                        wait("acc_ready", at("acc_ready", 2))
                        with act.Fori(0, E) as e:
                            for m in range(NC):
                                act.wait_ge(S["x_mm"], at("x_mm", 2 * e + m + 1))
                                nc.scalar.activation(ge[:, m], pq[m][:, :], ACT.Gelu,
                                                     bias=b_e[:, TOP, m:m + 1]).then_inc(S["x_ge"], 1)
                    with act.Else():
                        act.sem_inc(S["x_ge"], 2 * E)

            walk(act, run)

        @block.vector
        def _(dve):
            wait = waiter(dve)
            dve.wait_ge(w_in[1], 16)
            dve.wait_ge(S["pt_full0"], 1)
            nc.vector.tensor_tensor(col[:, 8:8 + 3 * NC + NM], col[:, 8:8 + 3 * NC + NM],
                                    pt[0][:, 0:3 * NC + NM], ALU.add).then_inc(S["pt_free0"], 1)
            for n in range(3):
                for c in range(NC):
                    nc.vector.tensor_scalar(w_qkv[:, n, c], w_qkv[:, n, c], ln1w[:, c:c + 1], None, ALU.mult)
            for c in range(NC):
                last = nc.vector.tensor_scalar(w_fc32[:, c], w_fc32[:, c], ln2w[:, c:c + 1], None, ALU.mult)
            last.then_inc(fold_done, 1)
            dve.wait_ge(w_in[3], 16)
            dve.wait_ge(w_in[4], 16)
            dve.wait_ge(const_done, 4)

            def run(p):
                at = p.at
                links = [0]

                def link(ins):
                    links[0] += 1
                    ins.then_inc(S["dve_chain"], 1)
                    wait("dve_chain", at("dve_chain", links[0]))

                def transposed():
                    wait("pt_free0", at("pt_free0"))
                    wait("pt_free1", at("pt_free1"))

                def hold():
                    nc.vector.memset(held_at[:, :], 0.0)

                def stats(src, into):
                    hold()
                    for s in range(SUB):
                        last = nc.vector.bn_stats(stat[:, s], src[:, s])
                    link(last)
                    hold()
                    for s in range(SUB):
                        last = nc.vector.bn_aggr(into[:, s], stat[:, s])
                    link(last)

                def normed(dst, src, mean, rstd):
                    for s in range(SUB):
                        last = nc.vector.tensor_scalar(dst[:, s], src[:, s], mean(s), rstd(s), ALU.subtract, ALU.mult)
                    return last

                if p.stage in ("DS", "D1", "Y"):
                    slot = p.t % RING
                    m1 = mv1[:, slot]
                    r1 = rs1[:, slot]
                if p.stage == "DS":
                    wait("x_in", at("x_in"))
                    stats(x_sb[:, slot], mv)
                    nc.vector.tensor_copy(m1, mv[:, :, :])
                    nc.vector.tensor_scalar(var2[:, 0], mv[:, :, 1], 1.0 + EPS, EPS * EPS, ALU.mult, ALU.add)
                    nc.vector.tensor_scalar(var2[:, 1], mv[:, :, 1], EPS, None, ALU.add).then_inc(S["var_ready"], 1)
                if p.stage == "D1":
                    wait("rstd_ready", at("rstd_ready"))
                    wait("s_ready", at("s_ready"))
                    transposed()
                    normed(xhat, x_sb[:, slot], lambda s: m1[:, s, 0:1], lambda s: r1[:, 0, s:s + 1]).then_inc(S["xhat_ready"], 1)
                    if isinstance(p.t, int) and p.t == 0:
                        dve.wait_ge(fold_done, 1)
                        dve.wait_ge(w_in[6], 16)
                        dve.wait_ge(w_in[7], 16)
                        for n, (w, w32) in enumerate(((w_fc, w_fc32), (w_o, w_o32), (w_pj, w_pj32))):
                            nc.vector.tensor_copy(w[:, 0], w32).then_inc(split_done, 1)
                            dve.wait_ge(split_done, 2 * n + 1)
                            nc.vector.tensor_tensor(w[:, 1], w32, w[:, 0].bitcast(f32), ALU.subtract).then_inc(split_done, 1)
                if p.stage == "D2":
                    wait("out_stored", at("out_stored"))
                    for j in range(2 * NC):
                        if j % NC == 0:
                            c = "qk"[j // NC]
                            wait(f"{c}_out", at(f"{c}_out"))
                        _, full, k = qk_bank(j)
                        free = full.replace("full", "free")
                        wait(free, at(free, k))
                        nc.vector.scalar_tensor_tensor(relub[:, j % 2], expb[:, j % 2], 1.0, relub[:, j % 2],
                                                       ALU.min, ALU.add).then_inc(S["feat_ready"], 1)
                        part = feat[:, j // NC, j % NC]
                        wait("feat_ready", at("feat_ready", 3 * j + 1))
                        nc.vector.tensor_copy(part[:, 0], relub[:, j % 2]).then_inc(S["feat_ready"], 1)
                        wait("feat_ready", at("feat_ready", 3 * j + 2))
                        nc.vector.tensor_tensor(part[:, 1], relub[:, j % 2], part[:, 0].bitcast(f32),
                                                ALU.subtract).then_inc(S["feat_ready"], 1)
                if p.stage in ("B0", "B"):
                    for r in range(ROUNDS)[slice(0, 1) if p.stage == "B0" else slice(1, None)]:
                        for u in range(2):
                            for h in range(2):
                                if r >= 1 and h == 0:
                                    wait("am_used", at("am_used", 2 * (r - 1) + u + 1))
                                if r >= 1 and h == 1:
                                    wait(f"pq_full{u}", at(f"pq_full{u}", r))
                                wait(f"ps_full{u}", at(f"ps_full{u}", 2 * (r - (p.stage == "B")) + h + 1))
                                nc.vector.tensor_tensor(am[:, 2 * u + h].rearrange("p (g n) -> p g n", n=P),
                                                        ps[u][h][:, :].rearrange("p (g n) -> p g n", n=P),
                                                        mask[:, :].unsqueeze(1).broadcast_to([P, RG // 2, P]),
                                                        ALU.mult).then_inc(S[f"ps_free{u}"], 1)
                if p.stage == "H":
                    for c in range(NC):
                        wait("h_round", at("h_round", c + 1))
                        nc.vector.tensor_tensor(hT[:, 1, c], pt[c][:, :], hT[:, 0, c].bitcast(f32),
                                                ALU.subtract).then_inc(S[f"pt_free{c}"], 1)
                if p.stage in UP:
                    for k, m in hidden_chunks(p):
                        wait(f"pq_free{m % 2}", at(f"pq_free{m % 2}", k // 2 + 1))
                        nc.vector.tensor_tensor(hidden[:, 1, m], gelub[:, m % 2], hidden[:, 0, m].bitcast(f32),
                                                ALU.subtract).then_inc(S["rest_ready"], 1)
                if p.stage == "A1":
                    wait("den_in", at("den_in"))
                    link(nc.vector.tensor_scalar(den[:, :], den[:, :], DEN_EPS, None, ALU.add))
                    nc.vector.reciprocal(den[:, :], den[:, :]).then_inc(S["rden_ready"], 1)
                if p.stage == "N":
                    wait("num_in", at("num_in"))
                    wait("rden_in", at("rden_in"))
                    link(nc.vector.tensor_tensor(num, num, rden.unsqueeze(1).broadcast_to([P, NC, T]), ALU.mult))
                    link(nc.vector.tensor_copy(attnT[:, 0], num))
                    nc.vector.tensor_tensor(attnT[:, 1], num, attnT[:, 0].bitcast(f32), ALU.subtract).then_inc(S["attnT_ready"], 1)
                if p.stage == "Y":
                    wait("s_ready", at("s_ready"))
                    transposed()
                    normed(x1, x_sb[:, slot], lambda s: m1[:, s, 0:1], lambda s: r1[:, 1, s:s + 1]).then_inc(S["y_ready"], 1)
                if p.stage == "A2":
                    wait("yb_ready", at("yb_ready"))
                    for u in range(2):
                        wait("ps_full1", at("ps_full1", u + 1))
                        o = x1[:, 2 * u:2 * u + 2].rearrange("p s d -> p (s d)")
                        nc.vector.tensor_tensor(o, o, ps[1][u][:, :], ALU.add).then_inc(S["ps_free1"], 1)
                    wait("ps_free1", at("ps_free1", 2))
                    stats(x1, mv)
                    nc.vector.tensor_scalar(var2[:, 0], mv[:, :, 1], EPS, None, ALU.add).then_inc(S["var_ready"], 1)
                if p.stage == "R":
                    wait("rstd_ready", at("rstd_ready"))
                    transposed()
                    normed(hn, x1, lambda s: mv[:, s, 0:1], lambda s: rs[:, s:s + 1]).then_inc(S["h_ready"], 1)
                if p.stage == "J":
                    wait("s_ready", at("s_ready"))
                    x2 = x2_sb[:, p.t % RING]
                    for s in range(2):
                        for u in range(2):
                            full, k = ("ps_full0", u + 1) if s == 0 else (f"pq_full{u}", 1)
                            wait(full, at(full, k))
                            nc.vector.tensor_tensor(x2[:, 2 * u + s], down_bank(u, s)[:, 0:D], x_sb[:, p.t % RING, 2 * u + s],
                                                    ALU.add).then_inc(S[full.replace("full", "free")], 1)
                    for name, k in (("ps_free0", 2), ("pq_free0", 1), ("pq_free1", 1)):
                        wait(name, at(name, k))
                    stats(x2, mv)
                    nc.vector.tensor_scalar(var2[:, 0], mv[:, :, 1], EPS, None, ALU.add).then_inc(S["var_ready"], 1)
                    wait("rstd_ready", at("rstd_ready", 1))
                    transposed()
                    normed(z, x2, lambda s: mv[:, s, 0:1], lambda s: rs[:, s:s + 1]).then_inc(S["z_ready"], 1)
                if p.stage == "G":
                    transposed()
                    link(nc.vector.reduce_sum(gs[:, 0:NC], pooled[:, :, :], AX))
                    for c in range(NC):
                        last = nc.vector.tensor_copy(pb128[:, c], gs[:, c:c + 1].broadcast_to([P, P]))
                    last.then_inc(S["pool_ready"], 1)
                    wait("pt_full0", at("pt_full0", 1))
                    link(nc.vector.scalar_tensor_tensor(g8[:, LOGIT], pt[0][:, 0:E], 1.0 / SEQ, row[:, 2 * D:2 * D + E],
                                                        ALU.mult, ALU.add))
                    hold()
                    link(nc.vector.max(g8[:, TOP8], g8[:, LOGIT]))
                    nc.vector.tensor_scalar(g8[:, SHIFTED], g8[:, LOGIT], g8[:, TOP8, 0:1], None,
                                            ALU.subtract).then_inc(S["logit_ready"], 1)
                    link(nc.vector.tensor_scalar(g8[:, CHOSEN], g8[:, LOGIT], g8[:, TOP8, 1:2], None, ALU.is_ge))
                    link(nc.vector.tensor_tensor(g8[:, RANK], g8[:, CHOSEN], row[:, 2 * D + E:2 * D + 2 * E], ALU.mult))
                    hold()
                    link(nc.vector.max(g8[:, RANK8], g8[:, RANK]))
                    nc.vector.tensor_scalar(choice[:, 0:TOP], g8[:, RANK8, 0:TOP], -1.0, float(E), ALU.mult, ALU.add)
                    link(nc.vector.tensor_scalar(choice[:, TOP:TOP + 1], g8[:, RANK8, TOP:TOP + 1], 0.0, None, ALU.is_gt))
                    link(nc.vector.tensor_scalar(choice[:, 0:TOP], choice[:, 0:TOP], float(E - 1), None, ALU.min))
                    wait("out_stored", at("out_stored"))
                    wait("chosen_in", at("chosen_in"))
                    nc.vector.tensor_copy(choice_i[:, 0:3], choice[:, 0:3]).then_inc(S["choice_ready"], 1)
                    wait("gexp_ready", at("gexp_ready", 1))
                    link(nc.vector.tensor_tensor(g8[:, EXP], g8[:, EXP], g8[:, CHOSEN], ALU.mult))
                    link(nc.vector.reduce_sum(gs[:, 2:3], g8[:, EXP], AX))
                    link(nc.vector.reciprocal(gs[:, 3:4], gs[:, 2:3]))
                    link(nc.vector.tensor_scalar(g8[:, GATE], g8[:, EXP], gs[:, 3:4], None, ALU.mult))
                    nc.vector.scalar_tensor_tensor(g8[:, REST], g8[:, RANK], g8[:, RANK8, TOP - 1:TOP], g8[:, GATE],
                                                   ALU.is_lt, ALU.mult)
                    for n in range(TOP):
                        last = nc.vector.scalar_tensor_tensor(g8[:, ONE + n], g8[:, RANK], g8[:, RANK8, n:n + 1],
                                                              g8[:, GATE], ALU.is_equal, ALU.mult)
                    link(last)
                    nc.vector.reduce_sum(gtop[:, :], g8[:, ONE:ONE + TOP], AX).then_inc(S["pt_free0"], 1)
                if p.stage == "F1":
                    wait("pt_free0", at("pt_free0"))
                    wait("k_out", at("k_out"))
                    for m in range(NC):
                        wait(f"pq_free{m}", at(f"pq_free{m}", 1))
                        nc.vector.tensor_scalar(acc[:, m], ge[:, m], gtop[:, 0:1], None, ALU.mult).then_inc(S["acc_ready"], 1)
                if p.stage == "FX":
                    for m in range(NC):
                        wait(f"pq_free{m}", at(f"pq_free{m}"))
                        wait("acc_ready", at("acc_ready", m - 1))
                        nc.vector.scalar_tensor_tensor(acc[:, m], ge[:, m], gtop[:, 1:2], acc[:, m],
                                                       ALU.mult, ALU.add).then_inc(S["acc_ready"], 1)
                    more = more_chosen(dve)
                    with dve.If(more > 0):
                        with dve.Fori(0, E) as e:
                            for m in range(NC):
                                dve.wait_ge(S["x_ge"], at("x_ge", 2 * e + m + 1))
                                nc.vector.scalar_tensor_tensor(acc[:, m], ge[:, m], g8[:, REST, bass.ds(e, 1)], acc[:, m],
                                                               ALU.mult, ALU.add).then_inc(S["x_sum"], 1)
                    with dve.Else():
                        dve.sem_inc(S["x_sum"], 2 * E)
                if p.stage == "F2":
                    wait("q_out", at("q_out"))
                    wait("out_stored", at("out_stored"))
                    for u in range(2):
                        wait(f"pt_full{u}", at(f"pt_full{u}", 1))
                        nc.vector.tensor_tensor(out_sb[:, 2 * u:2 * u + 2], pt[u][:, :].rearrange("p (s d) -> p s d", d=D),
                                                x2_sb[:, p.t % RING, 2 * u:2 * u + 2], ALU.add).then_inc(S[f"pt_free{u}"], 1)

            walk(dve, run)

        @block.tensor
        def _(pe):
            wait = waiter(pe)
            for n in (0, 1, 2, 5):
                pe.wait_ge(w_in[n], 16)
            for n in range(3 * NC + NM):
                for c in range(NC):
                    if n < 3 * NC:
                        w, b = w_qkv[:, n // NC, c, P * (n % NC):P * (n % NC + 1)], ln1b[:, c:c + 1]
                    else:
                        w, b = w_fc32[:, c, P * (n - 3 * NC):P * (n - 3 * NC + 1)], ln2b[:, c:c + 1]
                    last = nc.tensor.matmul(pt[0][:, n:n + 1], w, b, start=(c == 0), stop=(c == NC - 1))
            last.then_inc(S["pt_full0"], 1)
            pe.wait_ge(fold_done, 1)
            for n in range(6, 9):
                pe.wait_ge(w_in[n], 16)

            def run(p):
                at = p.at

                def bank_q(n, k):
                    wait(f"pq_free{n}", at(f"pq_free{n}", k))

                def transposes(src):
                    for c in range(NC):
                        wait(f"pt_free{c}", at(f"pt_free{c}"))
                        for s in range(SUB):
                            last = nc.tensor.transpose(pt[c][:, P * s:P * (s + 1)], src[:, s, P * c:P * (c + 1)], ident[:, :])
                        last.then_inc(S[f"pt_full{c}"], 1)

                def expert(w, m):
                    for c in range(NC):
                        last = nc.tensor.matmul(pq[m][:, :], w[:, c, P * m:P * (m + 1)], zT[:, p.t % RING, c],
                                                start=(c == 0), stop=(c == NC - 1))
                    return last

                def copied(k):
                    for c in range(2):
                        wait(f"pt_free{c}", at(f"pt_free{c}", k))

                if p.stage == "X":
                    wait("xhat_ready", at("xhat_ready"))
                    transposes(xhat)
                if p.stage == "D2":
                    copied(0)
                    for j in (4, 5, 0, 1, 2, 3):
                        if j >= 2 * NC:
                            bank, full, k = pq[j % 2], f"pq_full{j % 2}", 1
                        else:
                            bank, full, k = qk_bank(j)
                        free = full.replace("full", "free")
                        wait(free, at(free, 0 if full == "ps_full1" else k - 1))
                        for c in range(NC):
                            last = nc.tensor.matmul(bank[:, :], w_qkv[:, j // NC, c, P * (j % NC):P * (j % NC + 1)],
                                                    xhT[:, c], start=(c == 0), stop=(c == NC - 1))
                        last.then_inc(S[full], 1)
                if p.stage == "W":
                    copied(0)
                    if isinstance(p.i, int) and p.i == 1:
                        pe.wait_ge(split_done, 6)
                    for _ in range(16):
                        nc.tensor.matmul(pt[0][:, :], w_fc[:, 0, 0, 0:P], w_fc[:, 0, 0, 0:512], start=True, stop=True)
                if p.stage == "VT":
                    wait("v_in", at("v_in"))
                    for u in range(4):
                        wait(f"pt_free{u % 2}", at(f"pt_free{u % 2}", u // 2))
                        for g in range(4):
                            last = nc.tensor.transpose(pt[u % 2][:, P * g:P * (g + 1)],
                                                       vd[:, :, :, :].rearrange("p h b t -> p (h b t)")[:, 4 * u + g::GG // 2], ident[:, :])
                        last.then_inc(S[f"pt_full{u % 2}"], 1)
                if p.stage in ("B0", "B"):
                    if p.stage == "B0":
                        copied(0)
                        wait("q_in", at("q_in"))
                        wait("k_in", at("k_in"))

                    def score(r, u, h, g):
                        rows, gg = slice(64 * h, 64 * h + KP), RG * r + g
                        lo = P * (g % (RG // 2))
                        return nc.tensor.matmul(ps[u][h][:, lo:lo + P], kd[rows, gg::GG], qd[rows, gg::GG],
                                                start=True, stop=True)

                    def weighted(r, h, g):
                        lo = P * (g % (RG // 2))
                        return nc.tensor.matmul(pq[g // (RG // 2)][32 * h:32 * h + 32, lo:lo + P], vb[:, GG * h + RG * r + g],
                                                am[:, 2 * (g // (RG // 2)) + h, lo:lo + P], start=True, stop=True)

                    for r in range(ROUNDS + 1)[slice(0, 1) if p.stage == "B0" else slice(1, None)]:
                        for u in range(2):
                            if r >= 1:
                                bank_q(u, r - 1)
                            for h in range(2):
                                if p.stage == "B0":
                                    wait(f"ps_free{u}", at(f"ps_free{u}"))
                                else:
                                    wait(f"ps_free{u}", at(f"ps_free{u}", 2 * (r - 1) + h - 1))
                                for g in range(RG // 2 * u, RG // 2 * (u + 1)):
                                    if r < ROUNDS:
                                        last = score(r, u, h, g)
                                        if g % (RG // 2) == RG // 2 - 1:
                                            last.then_inc(S[f"ps_full{u}"], 1)
                                    if r >= 1:
                                        last = weighted(r - 1, h, g)
                                if r >= 1:
                                    last.then_inc(S["am_used" if h == 0 else f"pq_full{u}"], 1)
                if p.stage == "A2":
                    wait("attnT_ready", at("attnT_ready"))
                    wait("ps_free1", at("ps_free1"))
                    for u in range(2):
                        for s in range(2):
                            for c in range(NC):
                                lo = P * (2 * u + s)
                                for n, (a, b) in enumerate(TERMS):
                                    last = nc.tensor.matmul(ps[1][u][:, D * s:D * (s + 1)], attnT[:, a, c, lo:lo + P],
                                                            w_o[:, b, c], start=(c == 0 and n == 0),
                                                            stop=(c == NC - 1 and n == len(TERMS) - 1))
                        last.then_inc(S["ps_full1"], 1)
                if p.stage == "H":
                    wait("h_ready", at("h_ready"))
                    transposes(hn)
                if p.stage in UP:
                    for k, m in hidden_chunks(p):
                        bank_q(m % 2, k // 2)
                        order = [(a, b, c) for a, cb in ((0, (0, 1)), (1, (0,))) for c in range(NC) for b in cb]
                        for n, (a, b, c) in enumerate(order):
                            if m == 0 and b == 0:
                                if a == 0:
                                    wait("h_round", at("h_round", c - NC + 1))
                                else:
                                    wait(f"pt_free{c}", at(f"pt_free{c}"))
                            last = nc.tensor.matmul(pq[m % 2][:, :], w_fc[:, b, c, P * m:P * (m + 1)], hT[:, a, c],
                                                    start=(n == 0), stop=(n == len(order) - 1))
                        last.then_inc(S[f"pq_full{m % 2}"], 1)
                if p.stage == "J":
                    wait("rest_ready", at("rest_ready"))
                    wait("ps_free0", at("ps_free0"))
                    for ab in sorted(TERMS, reverse=True):
                        a, b = ab
                        for s in range(2):
                            for u in range(2):
                                lo = P * (2 * u + s)
                                if ab == (1, 0) and s == 1:
                                    bank_q(u, 0)
                                for m in range(NM):
                                    last = nc.tensor.matmul(down_bank(u, s)[:, 0:D], hidden[:, a, m, lo:lo + P],
                                                            w_pj[:, b, m], start=(ab == (1, 0) and m == 0),
                                                            stop=(ab == (0, 0) and m == NM - 1))
                                if ab == (0, 0):
                                    last.then_inc(S["ps_full0" if s == 0 else f"pq_full{u}"], 1)
                        if a == 1:
                            last.then_inc(S["rest_used"], 1)
                if p.stage == "E":
                    wait("z_ready", at("z_ready"))
                    transposes(z)
                if p.stage == "G":
                    wait("pool_ready", at("pool_ready", 1))
                    wait("pt_free0", at("pt_free0"))
                    for c in range(NC):
                        last = nc.tensor.matmul(pt[0][:, 0:E], pb128[:, c], w_g[:, c], start=(c == 0), stop=(c == NC - 1))
                    last.then_inc(S["pt_full0"], 1)
                if p.stage == "F1":
                    copied(-1)
                    wait("chosen_in", at("chosen_in"))

                    for e in range(TOP):
                        for m in range(NC):
                            bank_q(m, e)
                            expert(w_e[:, e], m).then_inc(S[f"pq_full{m}"], 1)
                if p.stage == "FX":
                    more = more_chosen(pe)
                    with pe.If(more > 0):
                        bank_q(0, 0)
                        bank_q(1, 0)
                        pe.sem_inc(held, 1)
                        with pe.Fori(0, E) as e:
                            pe.wait_ge(S["xw_in"], at("xw_in", 32 * e + 32))
                            pe.wait_ge(S["x_sum"], at("x_sum", 2 * e))
                            for m in range(NC):
                                expert(w_x, m).then_inc(S["x_mm"], 1)
                        wait("x_sum", at("x_sum", 2 * E))
                    with pe.Else():
                        pe.sem_inc(S["x_mm"], 2 * E)
                if p.stage == "F2":
                    wait("acc_ready", at("acc_ready"))
                    for u in range(2):
                        wait(f"pt_free{u}", at(f"pt_free{u}"))
                        for s in range(2):
                            for m in range(NC):
                                lo = P * (2 * u + s)
                                last = nc.tensor.transpose(pt[u][:, D * s + P * m:D * s + P * (m + 1)],
                                                           acc[:, m, lo:lo + P], ident[:, :])
                        last.then_inc(S[f"pt_full{u}"], 1)

            walk(pe, run)


def kernel(**inputs):
    import concourse.bacc as bacc
    from concourse.bass_utils import run_bass_kernel_spmd

    get = {k.replace("L0_", ""): np.asarray(v) for k, v in inputs.items()}

    def chunks(w):
        return np.moveaxis(w.reshape(-1, P, *w.shape[1:]), 1, 0)

    def heads_inner(w):
        return np.swapaxes(w.reshape(*w.shape[:-1], H, HD), -1, -2).reshape(w.shape)

    arrays = {
        "x": get["attn_q_x"].reshape(BATCH * SEQ, D),
        "wqkv": np.stack([chunks(heads_inner(get["attn_wq"])), chunks(heads_inner(get["attn_wk"])), chunks(get["attn_wv"])], 1),
        "wo": chunks(get["attn_wo"].reshape(H, HD, D).transpose(1, 0, 2).reshape(D, D)),
        "fcw": chunks(get["attn_fc_w"]),
        "pjw": chunks(get["attn_proj_w"]),
        "gw": chunks(get["ffn_gate_w"].T),
        "ew": np.stack([chunks(w.T) for w in get["ffn_expert_w"]], 1),
        "eb": np.stack([chunks(b) for b in get["ffn_expert_b"]], 1),
        "cols": np.concatenate([chunks(heads_inner(get[n]) if n in ("attn_bq", "attn_bk") else get[n]) for n in (
            "attn_ln1_w", "attn_ln1_b", "attn_ln2_w", "attn_ln2_b", "attn_bq", "attn_bk", "attn_bv", "attn_fc_b")], 1),
        "rows": np.tile(np.concatenate([get["attn_bo"], get["attn_proj_b"], get["ffn_gate_b"],
                                         np.arange(E, 0, -1, dtype=np.float32)])[None], (P, 1)),
        "ident": np.eye(P, dtype=np.float32),
        "mask": (np.arange(P)[:, None] % (2 * TB) == np.arange(P)[None] % (2 * TB)).astype(np.float32),
    }
    nc = bacc.Bacc("TRN2", target_bir_lowering=False, num_devices=1)
    maps, args = {}, []
    for name, a in arrays.items():
        a = np.ascontiguousarray(a)
        maps[f"in_{name}"] = a
        args.append(nc.dram_tensor(f"in_{name}", a.shape, mybir.dt.from_np(a.dtype), kind="ExternalInput").ap())
    out = nc.dram_tensor("out", (BATCH * SEQ, D), mybir.dt.float32, kind="ExternalOutput").ap()
    build(nc, *args, out)
    r = run_bass_kernel_spmd(nc, [maps], core_ids=[0])
    return r.results[0]["out"].reshape(BATCH, SEQ, D)
```
